# Optimizing a Trainium2 kernel written in Bass

```python
import numpy as np
import jax
import jax.numpy as jnp

def _softmax(x, axis=-1):
    return jax.nn.softmax(x, axis=axis)

def _gelu(x):
    return jax.nn.gelu(x, approximate=True)

def _silu(x):
    return jax.nn.silu(x)

def _sigmoid(x):
    return jax.nn.sigmoid(x)

def _layernorm(x, axis=-1, eps=1e-05):
    m = jnp.mean(x, axis=axis, keepdims=True)
    v = jnp.var(x, axis=axis, keepdims=True)
    return (x - m) / jnp.sqrt(v + eps)

def _scatter_add(tgt, idx, src, axis=0):
    return tgt.at[idx].add(src)

def _segment_sum(src, seg, n):
    return jax.ops.segment_sum(src, seg, n)
kernel_name = 'mk_adj_ffn_d1_adj_r2_eef210'

def setup_inputs(seed: int=0):
    np.random.seed(seed)
    _w = jnp.asarray

    def _rec_inputs():
        import jax
        import jax.numpy as jnp
        _gk = jax.random.key(seed)
        x = -0.0005207 + 1.001 * jax.random.normal(jax.random.fold_in(_gk, 1), (4096, 128), jnp.float32)
        _a = jax.random.bernoulli(jax.random.fold_in(_gk, 2), 0.000976562, (4096, 4096))
        _a = jnp.logical_or(_a, jnp.swapaxes(_a, -1, -2))
        _a = jnp.logical_or(_a, jnp.eye(4096, dtype=bool))
        _af = _a.astype(jnp.float32)
        adj = _af
        return (x, adj)
    x, adj = _rec_inputs()

    def _L0_gnn_setup():
        import jax, jax.numpy as jnp
        import numpy as np
        N = 4096
        IN_DIM = 256
        HID = 128
        REL_DIM = 128
        key = jax.random.key(seed)
        ks = jax.random.split(key, 8)
        s = 1.0 / np.sqrt(IN_DIM)
        return {'relation': jax.random.normal(ks[0], (N, REL_DIM), dtype=jnp.float32), 'context': jax.random.normal(ks[1], (N, IN_DIM), dtype=jnp.float32), 'adj_tensor': jax.random.randint(ks[2], (N, N), 0, 2).astype(jnp.float32), 'W_common': jax.random.normal(ks[3], (HID, IN_DIM), dtype=jnp.float32) * s, 'w_left': jax.random.normal(ks[4], (HID,), dtype=jnp.float32) * (1.0 / np.sqrt(HID)), 'b_left': jax.random.normal(ks[5], (), dtype=jnp.float32) * 0.01, 'w_right': jax.random.normal(ks[6], (HID,), dtype=jnp.float32) * (1.0 / np.sqrt(HID)), 'b_right': jax.random.normal(ks[7], (), dtype=jnp.float32) * 0.01}
    _L0_gnn_all = _L0_gnn_setup()
    _L0_gnn_in = {k: v for k, v in _L0_gnn_all.items() if k in ('context', 'W_common', 'w_left', 'b_left', 'w_right', 'b_right')}
    del _L0_gnn_all

    def _L0_ffn_setup():
        import jax, jax.numpy as jnp
        import numpy as np
        TOP_K = 2
        LN_EPS = 1e-05
        key = jax.random.key(seed)
        ks = jax.random.split(key, 8)
        B, S, D, E, H = (16, 512, 128, 8, 512)
        x = jax.random.normal(ks[0], (B, S, D), dtype=jnp.float32)
        Wr = jax.random.normal(ks[1], (D, E), dtype=jnp.float32) * 0.1
        br = jnp.zeros((E,), dtype=jnp.float32)
        ln_g = jnp.ones((E, D), dtype=jnp.float32)
        ln_b = jnp.zeros((E, D), dtype=jnp.float32)
        W1 = jax.random.normal(ks[2], (E, D, H), dtype=jnp.float32) * (1.0 / np.sqrt(D))
        b1 = jnp.zeros((E, H), dtype=jnp.float32)
        W2 = jax.random.normal(ks[3], (E, H, D), dtype=jnp.float32) * (1.0 / np.sqrt(H))
        b2 = jnp.zeros((E, D), dtype=jnp.float32)
        return {'x': x, 'Wr': Wr, 'br': br, 'ln_g': ln_g, 'ln_b': ln_b, 'W1': W1, 'b1': b1, 'W2': W2, 'b2': b2}
    _L0_ffn_all = _L0_ffn_setup()
    _L0_ffn_in = {k: v for k, v in _L0_ffn_all.items() if k in ('Wr', 'br', 'ln_g', 'ln_b', 'W1', 'b1', 'W2', 'b2')}
    del _L0_ffn_all
    return {'x': x, 'adj': adj, 'L0_gnn_context': _L0_gnn_in['context'], 'L0_gnn_W_common': _L0_gnn_in['W_common'], 'L0_gnn_w_left': _L0_gnn_in['w_left'], 'L0_gnn_b_left': _L0_gnn_in['b_left'], 'L0_gnn_w_right': _L0_gnn_in['w_right'], 'L0_gnn_b_right': _L0_gnn_in['b_right'], 'L0_ffn_Wr': _L0_ffn_in['Wr'], 'L0_ffn_br': _L0_ffn_in['br'], 'L0_ffn_ln_g': _L0_ffn_in['ln_g'], 'L0_ffn_ln_b': _L0_ffn_in['ln_b'], 'L0_ffn_W1': _L0_ffn_in['W1'], 'L0_ffn_b1': _L0_ffn_in['b1'], 'L0_ffn_W2': _L0_ffn_in['W2'], 'L0_ffn_b2': _L0_ffn_in['b2']}

def reference(x, adj, L0_gnn_context, L0_gnn_W_common, L0_gnn_w_left, L0_gnn_b_left, L0_gnn_w_right, L0_gnn_b_right, L0_ffn_Wr, L0_ffn_br, L0_ffn_ln_g, L0_ffn_ln_b, L0_ffn_W1, L0_ffn_b1, L0_ffn_W2, L0_ffn_b2):
    import jax
    import jax.numpy as jnp

    def _L0_gnn_ref(relation, context, adj_tensor, W_common, w_left, b_left, w_right, b_right):
        import jax, jax.numpy as jnp
        import numpy as np
        N = 4096
        IN_DIM = 256
        HID = 128
        REL_DIM = 128
        in_fts = context @ W_common.T
        left = in_fts @ w_left + b_left
        right = in_fts @ w_right + b_right
        logits = left[:, None] + right[None, :]
        logits = jnp.where(logits >= 0, logits, 0.2 * logits)
        logits = jnp.where(adj_tensor <= 0.0, -jnp.inf, logits)
        coefs = jax.nn.softmax(logits, axis=-1)
        x = coefs @ relation
        return jax.nn.relu(x)

    def _L0_ffn_ref(x, Wr, br, ln_g, ln_b, W1, b1, W2, b2):
        import jax, jax.numpy as jnp
        import numpy as np
        TOP_K = 2
        LN_EPS = 1e-05
        B, S, D = x.shape
        N = B * S
        xt = x.reshape(N, D)
        logits = xt @ Wr + br
        probs = jax.nn.softmax(logits, axis=-1)
        top_p, top_idx = jax.lax.top_k(probs, TOP_K)
        weights = top_p / top_p.sum(axis=-1, keepdims=True)
        mu = xt.mean(axis=-1, keepdims=True)
        var = ((xt - mu) ** 2).mean(axis=-1, keepdims=True)
        xn = (xt - mu) * jax.lax.rsqrt(var + LN_EPS)
        xe = xn[None, :, :] * ln_g[:, None, :] + ln_b[:, None, :]
        h = jax.nn.gelu(jnp.einsum('end,edh->enh', xe, W1) + b1[:, None, :], approximate=False)
        y = jnp.einsum('enh,ehd->end', h, W2) + b2[:, None, :]
        y_tok = jnp.transpose(y, (1, 0, 2))
        sel = jnp.take_along_axis(y_tok, top_idx[:, :, None], axis=1)
        out = (weights[:, :, None] * sel).sum(axis=1)
        return out.reshape(B, S, D)
    x = x + _L0_gnn_ref(_layernorm(x, axis=-1), L0_gnn_context, adj, L0_gnn_W_common, L0_gnn_w_left, L0_gnn_b_left, L0_gnn_w_right, L0_gnn_b_right)
    x = x + _L0_ffn_ref(_layernorm(x, axis=-1)[None], L0_ffn_Wr, L0_ffn_br, L0_ffn_ln_g, L0_ffn_ln_b, L0_ffn_W1, L0_ffn_b1, L0_ffn_W2, L0_ffn_b2)[0]
    return x

_drawn_inputs = setup_inputs


def setup_inputs(seed=0):
    import zlib

    import numpy as np

    out = dict(_drawn_inputs(seed))
    spreads = {'L0_ffn_br': (0.0, 0.1),
     'L0_ffn_ln_g': (1.0, 0.2),
     'L0_ffn_ln_b': (0.0, 0.1),
     'L0_ffn_b1': (0.0, 0.1),
     'L0_ffn_b2': (0.0, 0.1)}
    factors = {}
    for name, (base, spread) in spreads.items():
        noise = np.random.default_rng([zlib.crc32(name.encode()), seed]).standard_normal(out[name].shape)
        drawn = base * np.exp(spread * noise) if base else spread * noise
        out[name] = jnp.asarray(drawn.astype(out[name].dtype))
    for name, factor in factors.items():
        out[name] = (out[name] * factor).astype(out[name].dtype)
    return out
```

```python
import concourse.bass as bass
from concourse import mybir
from contextlib import ExitStack

FP32 = mybir.dt.float32
U32 = mybir.dt.uint32
ALU = mybir.AluOpType
ACT = mybir.ActivationFunctionType
AX_X = mybir.AxisListType.X

P = 128
N = 4096
D = 128
T = N // P
KC = 256 // P
IT = 4
G = T // IT
GI = IT * P
JC = 512
C = N // JC
JB = JC // P
RING = 4
NB = N // P
TB = 3
E = 8
H = 512
HB = H // P
DA = D + 1
SLOPE = 0.2
EPS = 1e-5


class Count:

    def __init__(self, engine, sem):
        self.engine, self.sem, self.base, self.n = engine, sem, 0, 0

    def __call__(self, instruction):
        instruction.then_inc(self.sem, 1)
        self.n += 1
        self.wait()

    def mark(self, instruction):
        instruction.then_inc(self.sem, 1)
        self.n += 1

    def wait(self):
        self.engine.wait_ge(self.sem, self.base + self.n)

    def enter(self, i, per_step):
        self.outside, self.per_step = self.base + self.n, per_step
        self.base, self.n = self.outside + i * per_step, 0

    def leave(self, steps):
        assert self.n == self.per_step, (self.n, self.per_step)
        self.base, self.n = self.outside + steps * self.per_step, 0


def build(nc, x, adj, context, W_common, w_left, b_left, w_right, b_right,
          Wr, br, ln_g, ln_b, W1, b1, W2, b2, out):
    ctx = ExitStack()
    with ctx:
        def sb(name, shape, dt=FP32):
            return ctx.enter_context(nc.sbuf_tensor(name, shape, dt))

        def sem(name):
            return ctx.enter_context(nc.semaphore(name))

        ring = sb("adj_ring", [P, RING, IT, JC])
        xt = sb("x_rows", [P, T, D])
        xh = sb("x_norm_aug", [P, T, DA])
        xn = sb("tokens_norm", [P, T, D])
        beta_row = sb("beta_row", [P, N])
        wide = sb("wide", [P, 2 * E * H])
        ctx_sb = wide[:, :].rearrange("p (t k) -> p t k", t=T)
        w1 = wide[:, 0:E * H].rearrange("p (e h) -> p e h", e=E)
        w2 = wide[:, E * H:2 * E * H].rearrange("p (e k d) -> p e k d", e=E, k=HB)
        b1_row = sb("b1_row", [P, E, H])
        b2_row = sb("b2_row", [P, E, D])
        gagg = sb("graph_sums", [P, T, DA])
        wbuf = sb("w_buf", [P, 4, GI])
        pbuf = sb("p_buf", [P, 4, GI])
        ident = sb("ident", [P, P])
        ones = sb("ones", [P, P])
        diag = sb("diag", [P, IT, P])
        wc_sb = sb("w_common", [P, KC * P])
        wlr = sb("w_left_right", [P, 2])
        wck = sb("w_folded", [P, KC, 2])
        blr = sb("b_left_right", [P, 2])
        ctxT = sb("context_T", [P, 2, IT, P])
        lr = sb("left_right", [P, T, 2])
        rmax = sb("r_max", [P, 4])
        uv = sb("u_v", [P, 2, T])
        beta = sb("beta", [P, T])
        stats = sb("stats", [P, T, 6])
        ms = sb("mean_scratch", [P, 6, T])
        half = sb("minus_half", [P, T])
        wr_sb = sb("w_router", [P, E])
        br_row = sb("br_row", [P, E])
        iota8 = sb("iota8", [P, E])
        y1 = sb("y1", [P, IT, D])
        yT = sb("yT", [P, GI])
        lg = sb("logits", [P, IT, E])
        top = sb("top", [P, IT, 8])
        topi = sb("topi", [P, IT, 8], U32)
        topf = sb("topf", [P, IT, 8])
        gw = sb("gate_w", [P, IT, 2])
        gs = sb("gate_s", [P, 4, IT, E])
        gates = sb("gates", [P, T, E])
        rden = sb("rden", [P, IT])
        hold = sb("hold", [P, 1])
        gcol = sb("ln_g_col", [P, E])
        bcol = sb("ln_b_col", [P, E])
        xs = sb("token_tile", [P, 2, D])
        xT = sb("token_tile_T", [P, 2, P])
        hb = ring[:, 0, 0:2]
        hg = ring[:, 1, 0:2]
        hT = ring[:, 2, 0:2]
        yb = sb("y_biased", [P, 2, D])
        gt = sb("gate_tile", [P, 2, E])
        yo = sb("y_out", [P, 2, D])

        ps = ctx.enter_context(nc.psum_tensor("psum", [P, 8, 512], FP32))

        ld_small, ld_ctx, ld_x, ld_w, ld_bias = (sem(s) for s in ("ld_small", "ld_ctx", "ld_x", "ld_w", "ld_bias"))
        adj_ld = [sem(f"adj_loaded{i}") for i in range(RING)]
        adj_used = sem("adj_used")
        consts = sem("consts_ready")
        dve_own, act_own, pool_own = sem("dve_own"), sem("act_own"), sem("pool_own")
        folded, folded_sb = sem("folded"), sem("folded_sb")
        ctxT_ps, ctxT_sb, ctxT_used = sem("ctxT_ps"), sem("ctxT_sb"), sem("ctxT_used")
        lr_ps, rowmax, allmax, u_ready, bexp_in, bexp = (sem(s) for s in ("lr_ps", "rowmax", "allmax", "u_ready", "beta_in", "beta_ready"))
        diag_ready, brow_ps, brow_sb = sem("diag_ready"), sem("brow_ps"), sem("brow_sb")
        var_ready, rstd_ready, xh_ready = sem("var_ready"), sem("rstd_ready"), sem("xh_ready")
        lnb_ps, bias_ready = sem("lnb_ps"), sem("bias_ready")
        turned, masked, p_free = sem("adj_turned"), sem("masked"), sem("p_free")
        sums_done, sums_free, sums_saved = sem("sums_done"), sem("sums_free"), sem("sums_saved")
        y_ready, yT_ps, yT_sb, lg_ps, lg_in, lg_exp = (sem(s) for s in ("y_ready", "yT_ps", "yT_sb", "lg_ps", "lg_in", "lg_exp"))
        routed = sem("routed")
        xs_ready, xs_turned, xT_sb, xT_used = sem("xs_ready"), sem("xs_turned"), sem("xT_sb"), sem("xT_used")
        h_ps, h_bias, h_gelu, h_turned, hT_sb, y_ps, y_taken = (sem(s) for s in ("h_ps", "h_bias", "h_gelu", "h_turned", "hT_sb", "y_ps", "y_taken"))
        tile_done, stored = sem("tile_done"), [sem(f"stored{k}") for k in range(2)]

        adj_v = adj.rearrange("(g i p) (c j) -> g c p i j", p=P, i=IT, j=JC)
        out_v = out.rearrange("(t p) d -> t p d", p=P)

        block = ctx.enter_context(nc.Block())

        @block.sync
        def _(sp):
            def load(g, c):
                sp.dma_start(ring[:, c % RING], adj_v[g, c]).then_inc(adj_ld[c % RING], 16)

            sp.dma_start(wlr[:, 0:1], w_left.rearrange("(h o) -> h o", o=1)).then_inc(ld_small, 16)
            sp.dma_start(wlr[:, 1:2], w_right.rearrange("(h o) -> h o", o=1)).then_inc(ld_small, 16)
            sp.dma_start(wc_sb[:], W_common).then_inc(ld_small, 16)
            for col, b in ((0, b_left), (1, b_right)):
                sp.dma_start(blr[:, col:col + 1], b.rearrange("(a o) -> a o", a=1).broadcast_to([P, 1])).then_inc(ld_small, 16)
            sp.dma_start(ctx_sb, context.rearrange("(t p) k -> p t k", p=P)).then_inc(ld_ctx, 16)
            sp.dma_start(xt[:], x.rearrange("(t p) d -> p t d", p=P)).then_inc(ld_x, 16)
            for c in range(RING):
                load(0, c)
            sp.wait_ge(ctxT_ps, T // 2)
            sp.dma_start(w1, W1.rearrange("e d h -> d e h")).then_inc(ld_w, 16)
            sp.dma_start(w2, W2.rearrange("e (k p) d -> p e k d", p=P)).then_inc(ld_w, 16)
            with sp.Fori(0, G - 1) as g:
                for c in range(C):
                    sp.wait_ge(turned, g * NB + (c + 1) * JB)
                    load(g + (1 if c >= C - RING else 0), (c + RING) % C)
            for c in range(C - RING):
                sp.wait_ge(turned, (G - 1) * NB + (c + 1) * JB)
                load(G - 1, c + RING)
            with sp.Fori(0, T // 2) as h:
                for k in range(2):
                    sp.wait_ge(tile_done, 2 * h + (k + 1))
                    sp.dma_start(out_v[2 * h + k], yo[:, k]).then_inc(stored[k], 16)
            for k in range(2):
                sp.wait_ge(stored[k], 16 * (T // 2) + 16)

        @block.gpsimd
        def _(pool):
            own = Count(pool, pool_own)
            own(nc.gpsimd.memset(ones[:], 1.0))
            nc.gpsimd.affine_select(out=ident[:], in_=ones[:], compare_op=ALU.is_equal, fill=0.0, base=0,
                                    pattern=[[-1, P]], channel_multiplier=1).then_inc(consts, 1)
            nc.gpsimd.memset(half[:], -0.5).then_inc(consts, 1)
            nc.gpsimd.iota(iota8[:], pattern=[[1, E]], base=0, channel_multiplier=0,
                           allow_small_or_imprecise_dtypes=True).then_inc(consts, 1)
            own(nc.gpsimd.memset(xh[:, :, D:DA], 1.0))
            nc.gpsimd.memset(pbuf[:, 0, 0:1], 0.0).then_inc(p_free, 4)
            nc.gpsimd.memset(pbuf[:, 0, 1:2], 0.0).then_inc(masked, TB)
            nc.gpsimd.memset(pbuf[:, 0, 2:3], 0.0).then_inc(sums_free, 1)
            for k in range(2):
                nc.gpsimd.memset(pbuf[:, 0, 3 + k:4 + k], 0.0).then_inc(stored[k], 16)
            pool.dma_start(wr_sb[:], Wr).then_inc(ld_bias, 16)
            with nc.allow_non_contiguous_dma(reason="1024 elements each"):
                pool.dma_start(gcol[:], ln_g.rearrange("e d -> d e")).then_inc(ld_bias, 16)
                pool.dma_start(bcol[:], ln_b.rearrange("e d -> d e")).then_inc(ld_bias, 16)
            pool.dma_start(br_row[:], br.rearrange("(a e) -> a e", a=1).broadcast_to([P, E])).then_inc(ld_bias, 16)
            pool.dma_start(b2_row[:].rearrange("p e d -> p (e d)"),
                           b2.rearrange("(a e) d -> a (e d)", a=1).broadcast_to([P, E * D])).then_inc(ld_bias, 16)
            pool.dma_start(b1_row[:].rearrange("p e h -> p (e h)"),
                           b1.rearrange("(a e) h -> a (e h)", a=1).broadcast_to([P, E * H])).then_inc(ld_bias, 16)
            pool.wait_ge(var_ready, 1)
            pool.wait_ge(consts, 2)
            nc.gpsimd.tensor_tensor(ms[:, 5, :], ms[:, 4, :], half[:], ALU.pow).then_inc(rstd_ready, 1)
            pool.wait_ge(rowmax, 1)
            nc.gpsimd.partition_all_reduce(rmax[:, 1:2], rmax[:, 0:1], P, bass.bass_isa.ReduceOp.max).then_inc(allmax, 1)
            with pool.Fori(0, G) as g:
                for k in range(2):
                    pool.wait_ge(var_ready, 2 * g + (k + 2))
                    nc.gpsimd.tensor_tensor(ms[:, 5, 0:IT], ms[:, 4, 0:IT], half[:, 0:IT], ALU.pow).then_inc(rstd_ready, 1)
            pool.wait_ge(routed, G)
            for k in range(2):
                nc.gpsimd.tensor_copy(gt[:, k], gates[:, k]).then_inc(xs_ready, 1)
                nc.gpsimd.tensor_copy(xs[:, k], xn[:, k]).then_inc(xs_ready, 1)
            with pool.Fori(0, T // 2 - 1) as h:
                for k in range(2):
                    pool.wait_ge(tile_done, 2 * h + (k + 1))
                    nc.gpsimd.tensor_copy(gt[:, k], gates[:, 2 * h + (k + 2)]).then_inc(xs_ready, 1)
                    nc.gpsimd.tensor_copy(xs[:, k], xn[:, 2 * h + (k + 2)]).then_inc(xs_ready, 1)

        @block.scalar
        def _(act):
            own = Count(act, act_own)
            for n in range(T // 2):
                act.wait_ge(ctxT_ps, n + 1)
                if n >= 2:
                    act.wait_ge(ctxT_used, n - 1)
                nc.scalar.activation(ctxT[:, n % 2].rearrange("p a b -> p (a b)"), ps[:, 5 + n % 2], ACT.Copy).then_inc(ctxT_sb, 1)
            act.wait_ge(allmax, 2)
            nc.scalar.activation(uv[:, 0], lr[:, :, 1], ACT.Exp, bias=rmax[:, 2:3]).then_inc(u_ready, 1)
            nc.scalar.activation(uv[:, 1], lr[:, :, 1], ACT.Exp, bias=rmax[:, 3:4], scale=SLOPE).then_inc(u_ready, 1)
            act.wait_ge(bexp_in, 1)
            nc.scalar.activation(beta[:], ms[:, 0, :], ACT.Exp, scale=SLOPE - 1.0).then_inc(bexp, 1)
            for g in range(G):
                act.wait_ge(brow_ps, g + 1)
                nc.scalar.activation(beta_row[:, g * GI:(g + 1) * GI], ps[:, 5 + g % 2], ACT.Copy).then_inc(brow_sb, 1)
            with act.Fori(0, G) as g:
                act.wait_ge(p_free, g * NB + (NB + 4))
                nc.scalar.activation(gagg[:, bass.ds(IT * g, IT)].rearrange("p (a b) d -> p a (b d)", a=2),
                                     ps[:, 0:2, 0:2 * DA], ACT.Copy).then_inc(sums_free, 1)
            act.wait_ge(sums_free, G + 1)
            nc.scalar.activation(rden[0:1, 0:1], ones[0:1, 0:1], ACT.Copy).then_inc(sums_saved, 1)
            with act.Fori(0, G) as g:
                act.wait_ge(yT_ps, g + 1)
                nc.scalar.activation(yT[:], ps[:, 5], ACT.Copy).then_inc(yT_sb, 1)
                act.wait_ge(lg_in, g + 1)
                nc.scalar.activation(lg[:].rearrange("p a e -> p (a e)"), gs[:, 0].rearrange("p a e -> p (a e)"), ACT.Exp).then_inc(lg_exp, 1)
            with act.Fori(0, T // 2) as h:
                for k in range(2):
                    act.wait_ge(xs_turned, 2 * h + (k + 1))
                    nc.scalar.activation(xT[:, k], ps[:, 7, 0:P], ACT.Copy).then_inc(xT_sb, 1)
                    for e in range(E):
                        s = (2 * h + k) * E + e
                        act.wait_ge(h_bias, s + 1)
                        nc.scalar.activation(hg[:, e % 2], hb[:, e % 2], ACT.Gelu).then_inc(h_gelu, 1)

        @block.vector
        def _(dve):
            own = Count(dve, dve_own)

            def centre(n):
                v = [stats[:, 0:n, k] for k in range(6)]
                m = [ms[:, k, 0:n] for k in range(6)]
                own.mark(nc.vector.tensor_tensor(m[0], v[1], v[4], ALU.add))
                own.mark(nc.vector.tensor_tensor(m[1], v[1], v[4], ALU.subtract))
                own(nc.vector.tensor_tensor(m[2], v[2], v[5], ALU.add))
                own.mark(nc.vector.tensor_scalar(m[3], m[0], 0.5, None, ALU.mult))
                own(nc.vector.tensor_tensor(m[5], m[1], m[1], ALU.mult))
                own(nc.vector.scalar_tensor_tensor(m[0], m[5], D / 4.0, m[2], ALU.mult, ALU.add))
                nc.vector.tensor_scalar(m[4], m[0], 1.0 / D, EPS, ALU.mult, ALU.add).then_inc(var_ready, 1)

            dve.wait_ge(ld_x, 16)
            for t in range(T):
                own.mark(nc.vector.bn_stats(stats[:, t], xt[:, t]))
            own.wait()
            centre(T)
            dve.wait_ge(rstd_ready, 1)
            for t in range(T):
                own.mark(nc.vector.tensor_scalar(xh[:, t, 0:D], xt[:, t], ms[:, 3, t:t + 1], ms[:, 5, t:t + 1],
                                                 ALU.subtract, ALU.mult))
            own.wait()
            dve.wait_ge(folded, 1)
            nc.vector.tensor_copy(wck[:].rearrange("p k o -> p (k o)"), ps[:, 7, 0:2 * KC]).then_inc(folded_sb, 1)
            dve.wait_ge(ctxT_used, T // 2)
            dve.wait_ge(ld_small, 5 * 16)
            for o in range(2):
                own.mark(nc.vector.tensor_scalar(lr[:, :, o], ps[:, 7, 2 * KC:2 * KC + 2 * T].rearrange("p (t o) -> p o t", o=2)[:, o],
                                                 blr[:, o:o + 1], None, ALU.add))
            own.wait()
            nc.vector.reduce_max(rmax[:, 0:1], lr[:, :, 1], AX_X).then_inc(rowmax, 1)
            dve.wait_ge(allmax, 1)
            own.mark(nc.vector.tensor_scalar(rmax[:, 2:3], rmax[:, 1:2], -1.0, None, ALU.mult))
            nc.vector.tensor_scalar(rmax[:, 3:4], rmax[:, 1:2], -SLOPE, None, ALU.mult).then_inc(allmax, 1)
            nc.vector.tensor_scalar(ms[:, 0, :], lr[:, :, 0], rmax[:, 1:2], 0.0, ALU.add, ALU.max).then_inc(bexp_in, 1)
            dve.wait_ge(bexp, 1)
            dve.wait_ge(consts, 1)
            for g in range(G):
                if g:
                    dve.wait_ge(brow_ps, g)
                for i in range(IT):
                    last = nc.vector.tensor_scalar(diag[:, i], ident[:], beta[:, g * IT + i:g * IT + i + 1], None, ALU.mult)
                    last.then_inc(diag_ready, 1)
            dve.wait_ge(u_ready, 2)
            dve.wait_ge(brow_sb, G)

            with dve.Fori(0, G) as g:
                own.enter(g, NB)

                def weigh(b):
                    own.mark(nc.vector.tensor_scalar(wbuf[:, b % 4], beta_row[:, bass.ds(g * GI, GI)],
                                                     uv[:, 1, b:b + 1], uv[:, 0, b:b + 1], ALU.mult, ALU.max))

                weigh(0)
                for b in range(NB):
                    dve.wait_ge(dve_own, own.base + (b + 1))
                    if b + 1 < NB:
                        dve.wait_ge(masked, g * NB + (b + TB - 2))
                        weigh(b + 1)
                    dve.wait_ge(turned, g * NB + (b + 1))
                    dve.wait_ge(p_free, g * NB + (b + 1))
                    nc.vector.scalar_tensor_tensor(pbuf[:, b % 4], ps[:, 2 + b % TB], 0.0, wbuf[:, b % 4],
                                                   ALU.is_gt, ALU.mult).then_inc(masked, 1)
                dve.wait_ge(masked, g * NB + (NB + TB))
                own.leave(G)

            dve.wait_ge(sums_saved, 1)
            dve.wait_ge(ld_bias, 6 * 16)
            with dve.Fori(0, G) as g:
                own.enter(g, 49)
                rows = bass.ds(IT * g, IT)
                own(nc.vector.reciprocal(rden[:], gagg[:, rows, D]))
                own(nc.vector.tensor_tensor(y1[:], gagg[:, rows, 0:D], rden[:].unsqueeze(2).broadcast_to([P, IT, D]), ALU.mult))
                own(nc.vector.scalar_tensor_tensor(xt[:, rows], y1[:], 0.0, xt[:, rows], ALU.max, ALU.add))
                nc.vector.memset(hold[:], 0.0)
                for i in range(IT):
                    own.mark(nc.vector.bn_stats(stats[:, i], xt[:, IT * g + i]))
                own.wait()
                centre(IT)
                dve.wait_ge(rstd_ready, 2 * g + 2)
                for i in range(IT):
                    own.mark(nc.vector.tensor_scalar(y1[:, i], xt[:, IT * g + i], ms[:, 3, i:i + 1], ms[:, 5, i:i + 1],
                                                     ALU.subtract, ALU.mult))
                own.wait()
                nc.vector.tensor_copy(rden[:, 0:1], ones[:, 0:1]).then_inc(y_ready, 1)
                nc.vector.memset(hold[:], 0.0)
                for i in range(IT):
                    own.mark(nc.vector.bn_stats(stats[:, i], y1[:, i]))
                own.wait()
                centre(IT)
                dve.wait_ge(rstd_ready, 2 * g + 3)
                for i in range(IT):
                    own.mark(nc.vector.tensor_scalar(xn[:, IT * g + i], y1[:, i], ms[:, 3, i:i + 1], ms[:, 5, i:i + 1],
                                                     ALU.subtract, ALU.mult))
                dve.wait_ge(lg_ps, g + 1)
                own(nc.vector.tensor_tensor(lg[:], ps[:, 6, 0:IT * E].rearrange("p (i e) -> p i e", i=IT),
                                            br_row[:].unsqueeze(1).broadcast_to([P, IT, E]), ALU.add))
                own(nc.vector.tensor_reduce(rden[:], lg[:], AX_X, ALU.max))
                nc.vector.tensor_tensor(gs[:, 0], lg[:], rden[:].unsqueeze(2).broadcast_to([P, IT, E]), ALU.subtract).then_inc(lg_in, 1)
                dve.wait_ge(lg_exp, g + 1)
                nc.vector.memset(hold[:], 0.0)
                for i in range(IT):
                    own.mark(nc.vector.max(top[:, i], lg[:, i]))
                own.wait()
                nc.vector.memset(hold[:], 0.0)
                for i in range(IT):
                    own.mark(nc.vector.max_index(topi[:, i], top[:, i], lg[:, i]))
                own.mark(nc.vector.tensor_tensor(rden[:], top[:, :, 0], top[:, :, 1], ALU.add))
                own.wait()
                own.mark(nc.vector.tensor_copy(topf[:], topi[:]))
                own(nc.vector.reciprocal(rden[:], rden[:]))
                own(nc.vector.tensor_tensor(gw[:], top[:, :, 0:2], rden[:].unsqueeze(2).broadcast_to([P, IT, 2]), ALU.mult))
                for k in range(2):
                    own(nc.vector.tensor_tensor(gs[:, k + 1], iota8[:].unsqueeze(1).broadcast_to([P, IT, E]),
                                                topf[:, :, k].unsqueeze(2).broadcast_to([P, IT, E]), ALU.is_equal))
                    own(nc.vector.tensor_tensor(gs[:, k + 1], gs[:, k + 1],
                                                gw[:, :, k].unsqueeze(2).broadcast_to([P, IT, E]), ALU.mult))
                nc.vector.tensor_tensor(gates[:, rows], gs[:, 1], gs[:, 2], ALU.add).then_inc(routed, 1)
                own.leave(G)

            for e in range(E):
                dve.wait_ge(lnb_ps, e + 1)
                own(nc.vector.tensor_tensor(b1_row[:, e], ps[:, 5 + e % 2], b1_row[:, e], ALU.add))
                nc.vector.tensor_scalar(w1[:, e], w1[:, e], gcol[:, e:e + 1], None, ALU.mult).then_inc(bias_ready, 1)

            with dve.Fori(0, T // 2) as h:
                own.enter(h, 2 * E * 2)
                for k in range(2):
                    t = 2 * h + k
                    for e in range(E):
                        s = t * E + e
                        dve.wait_ge(h_ps, s + 1)
                        nc.vector.tensor_tensor(hb[:, e % 2], ps[:, e % 2], b1_row[:, e], ALU.add).then_inc(h_bias, 1)
                        dve.wait_ge(h_turned, s + 1)
                        nc.vector.tensor_copy(hT[:, e % 2], ps[:, 2 + e % 2]).then_inc(hT_sb, 1)
                        dve.wait_ge(y_ps, s + 1)
                        ins = nc.vector.tensor_tensor(yb[:, e % 2], ps[:, 4 + e % 2, 0:D], b2_row[:, e], ALU.add)
                        own(ins)
                        src = xt[:, t] if e == 0 else yo[:, k]
                        if e == 0:
                            dve.wait_ge(xs_ready, 2 * t + 2)
                            dve.wait_ge(stored[k], 16 * h + 16)
                        last = nc.vector.scalar_tensor_tensor(yo[:, k], yb[:, e % 2], gt[:, k, e:e + 1], src, ALU.mult, ALU.add)
                        own(last)
                    nc.vector.tensor_copy(rden[:, 0:1], ones[:, 0:1]).then_inc(tile_done, 1)
                own.leave(T // 2)

        @block.tensor
        def _(pe):
            pe.wait_ge(ld_small, 5 * 16)
            for k in range(KC):
                last = nc.tensor.matmul(ps[:, 7, 2 * k:2 * k + 2], wc_sb[:, k * P:(k + 1) * P], wlr[:], start=True, stop=True)
            last.then_inc(folded, 1)
            pe.wait_ge(folded_sb, 1)
            pe.wait_ge(consts, 1)
            pe.wait_ge(ld_ctx, 16)

            def context_dot(n):
                pe.wait_ge(ctxT_sb, n + 1)
                for i in range(2):
                    for k in range(KC):
                        last = nc.tensor.matmul(ps[:, 7, 2 * KC + 2 * (2 * n + i):2 * KC + 2 * (2 * n + i) + 2],
                                                ctxT[:, n % 2, 2 * i + k], wck[:, k], start=(k == 0), stop=(k == KC - 1))
                last.then_inc(ctxT_used, 1)

            for n in range(T // 2):
                if n >= 2:
                    pe.wait_ge(ctxT_sb, n - 1)
                for i in range(2):
                    for k in range(KC):
                        last = nc.tensor.transpose(ps[:, 5 + n % 2, (2 * i + k) * P:(2 * i + k + 1) * P],
                                                   ctx_sb[:, 2 * n + i, k * P:(k + 1) * P], ident[:])
                last.then_inc(ctxT_ps, 1)
                if n:
                    context_dot(n - 1)
            context_dot(T // 2 - 1)
            for g in range(G):
                pe.wait_ge(diag_ready, IT * (g + 1))
                if g >= 2:
                    pe.wait_ge(brow_sb, g - 1)
                nc.tensor.matmul(ps[:, 5 + g % 2], ones[:], diag[:].rearrange("p a b -> p (a b)"), start=True, stop=True).then_inc(brow_ps, 1)

            def turn(g, b):
                c = b // JB
                if b % JB == 0:
                    pe.wait_ge(adj_ld[c % RING], 16 * (g * (C // RING) + (c // RING + 1)))
                pe.wait_ge(masked, g * NB + (b + 1))
                for i in range(IT):
                    last = nc.tensor.transpose(ps[:, 2 + b % TB, i * P:(i + 1) * P],
                                               ring[:, c % RING, i, (b % JB) * P:(b % JB + 1) * P], ident[:])
                last.then_inc(turned, 1)

            def add_up(g, b):
                pe.wait_ge(masked, g * NB + (b + 1 + TB))
                if b == 0:
                    pe.wait_ge(sums_free, g + 1)
                for i in range(IT):
                    at = ps[:, i // 2, (i % 2) * DA:(i % 2 + 1) * DA]
                    last = nc.tensor.matmul(at, pbuf[:, b % 4, i * P:(i + 1) * P], xh[:, b],
                                            start=(b == 0 and i % 2 == 0), stop=(b == NB - 1), skip_group_check=True)
                last.then_inc(p_free, 1)

            pe.wait_ge(rstd_ready, 1)
            pe.wait_ge(pool_own, 2)
            pe.wait_ge(brow_sb, G)
            with pe.Fori(0, G) as g:
                for b in range(2):
                    turn(g, b)
                for b in range(NB):
                    if b + 2 < NB:
                        turn(g, b + 2)
                    add_up(g, b)

            with pe.Fori(0, G) as g:
                pe.wait_ge(y_ready, g + 1)
                for i in range(IT):
                    last = nc.tensor.transpose(ps[:, 5, i * P:(i + 1) * P], y1[:, i], ident[:])
                last.then_inc(yT_ps, 1)
                pe.wait_ge(yT_sb, g + 1)
                for i in range(IT):
                    last = nc.tensor.matmul(ps[:, 6, i * E:(i + 1) * E], yT[:, i * P:(i + 1) * P], wr_sb[:], start=True, stop=True)
                last.then_inc(lg_ps, 1)

            pe.wait_ge(ld_w, 32)
            pe.wait_ge(routed, G)
            for e in range(E):
                if e >= 2:
                    pe.wait_ge(bias_ready, e - 1)
                nc.tensor.matmul(ps[:, 5 + e % 2], bcol[:, e:e + 1].broadcast_to([P, P]), w1[:, e], start=True, stop=True).then_inc(lnb_ps, 1)
            pe.wait_ge(bias_ready, E)

            with pe.Fori(0, T // 2) as h:
                for k in range(2):
                    t = 2 * h + k
                    pe.wait_ge(xs_ready, 2 * t + 2)
                    nc.tensor.transpose(ps[:, 7, 0:P], xs[:, k], ident[:]).then_inc(xs_turned, 1)
                    pe.wait_ge(xT_sb, t + 1)
                    for e in range(E):
                        s = t * E + e
                        nc.tensor.matmul(ps[:, e % 2], xT[:, k], w1[:, e], start=True, stop=True).then_inc(h_ps, 1)
                        pe.wait_ge(h_gelu, s + 1)
                        for j in range(HB):
                            last = nc.tensor.transpose(ps[:, 2 + e % 2, j * P:(j + 1) * P], hg[:, e % 2, j * P:(j + 1) * P], ident[:])
                        last.then_inc(h_turned, 1)
                        pe.wait_ge(hT_sb, s + 1)
                        for j in range(HB):
                            last = nc.tensor.matmul(ps[:, 4 + e % 2, 0:D], hT[:, e % 2, j * P:(j + 1) * P], w2[:, e, j],
                                                    start=(j == 0), stop=(j == HB - 1))
                        last.then_inc(y_ps, 1)


_INS = ['x', 'adj', 'L0_gnn_context', 'L0_gnn_W_common', 'L0_gnn_w_left', 'L0_gnn_b_left', 'L0_gnn_w_right',
        'L0_gnn_b_right', 'L0_ffn_Wr', 'L0_ffn_br', 'L0_ffn_ln_g', 'L0_ffn_ln_b', 'L0_ffn_W1', 'L0_ffn_b1',
        'L0_ffn_W2', 'L0_ffn_b2']


def kernel(**inputs):
    import numpy as np
    import concourse.bacc as bacc
    from concourse.bass_utils import run_bass_kernel_spmd

    nc = bacc.Bacc("TRN2", target_bir_lowering=False, num_devices=1)
    arrays, args = {}, []
    for name in _INS:
        a = np.ascontiguousarray(inputs[name])
        if a.ndim == 0:
            a = a.reshape(1)
        arrays[f"in_{name}"] = a
        args.append(nc.dram_tensor(f"in_{name}", a.shape, mybir.dt.from_np(a.dtype), kind="ExternalInput").ap())
    args.append(nc.dram_tensor("out", (N, D), FP32, kind="ExternalOutput").ap())
    build(nc, *args)
    r = run_bass_kernel_spmd(nc, [arrays], core_ids=[0])
    return r.results[0]["out"]
```

```python
import concourse.bass as bass
from concourse import mybir
from contextlib import ExitStack

FP32 = mybir.dt.float32
U32 = mybir.dt.uint32
ALU = mybir.AluOpType
BF16 = mybir.dt.bfloat16
I32 = mybir.dt.int32
ACT = mybir.ActivationFunctionType
AX_X = mybir.AxisListType.X

P = 128
N = 4096
D = 128
T = N // P
KC = 256 // P
IT = 4
G = T // IT
GI = IT * P
JC = 512
C = N // JC
JB = JC // P
RING = 4
NB = N // P
E = 8
H = 512
HB = H // P
DA = D + 1
SLOPE = 0.2
EPS = 1e-5
DEEP = 4
POST_T, POST_TWIN, POST_EXP = 11, 14, 18
POST_OWN = 49
PW = D + 2
REGION = N + P
NT = 72
PADS = E * REGION
SPARE = NT - 2 * T


class Count:

    def __init__(self, engine, sem):
        self.engine, self.sem, self.base, self.n = engine, sem, 0, 0

    def __call__(self, instruction):
        instruction.then_inc(self.sem, 1)
        self.n += 1
        self.wait()

    def mark(self, instruction):
        instruction.then_inc(self.sem, 1)
        self.n += 1

    def wait(self):
        self.engine.wait_ge(self.sem, self.base + self.n)

    def enter(self, i, per_step):
        self.outside, self.per_step = self.base + self.n, per_step
        self.base, self.n = self.outside + i * per_step, 0

    def leave(self, steps):
        assert self.n == self.per_step, (self.n, self.per_step)
        self.base, self.n = self.outside + steps * self.per_step, 0


def build(nc, x, adj, context, W_common, w_left, b_left, w_right, b_right,
          Wr, br, ln_g, ln_b, W1, b1, W2, b2, out):
    ctx = ExitStack()
    with ctx:
        def sb(name, shape, dt=FP32):
            return ctx.enter_context(nc.sbuf_tensor(name, shape, dt))

        def sem(name):
            return ctx.enter_context(nc.semaphore(name))

        routed_rows = nc.dram_tensor("routed_rows", (PADS + SPARE * P, PW), FP32, kind="Internal").ap()
        results = nc.dram_tensor("results", (2 * N + (E + SPARE) * P, D), FP32, kind="Internal").ap()

        ring = sb("adj_ring", [P, RING, IT, JC])
        mring = sb("mask_ring", [P, RING, IT, JC], BF16)
        xt = sb("x_rows", [P, T, D])
        xh = sb("x_norm_aug", [P, T, DA])
        beta_row = sb("beta_row", [P, GI])
        wide = sb("wide", [P, 2 * E * H])
        ctx_sb = wide[:, :].rearrange("p (t k) -> p t k", t=T)
        w1 = wide[:, 0:E * H]
        w2 = wide[:, E * H:2 * E * H]
        b1_row = sb("b1_row", [P, E * H])
        b2_row = sb("b2_row", [P, E * D])
        tbuf = sb("t_buf", [P, DEEP, GI])
        pbuf = sb("p_buf", [P, DEEP, GI])
        gsum = sb("graph_sums", [P, IT, DA])
        ident = sb("ident", [P, P])
        identb = sb("ident_bf16", [P, P], BF16)
        ones = sb("ones", [P, P])
        onesb = sb("ones_bf16", [P, P], BF16)
        before = sb("before", [P, P], BF16)
        diag = sb("diag", [P, IT, P])
        wc_sb = sb("w_common", [P, KC * P])
        wlr = sb("w_left_right", [P, 2])
        wck = sb("w_folded", [P, KC, 2])
        blr = sb("b_left_right", [P, 2])
        ctxT = sb("context_T", [P, 2, IT * P])
        lr = sb("left_right", [P, 2, T])
        rmax = sb("r_max", [P, 4])
        uv = sb("u_v_minus_u", [P, 3, T])
        lR = sb("left_plus_R", [P, T])
        beta = sb("beta", [P, T])
        stats = sb("stats", [P, T, 6])
        ms = sb("mean_scratch", [P, 6, T])
        half = sb("minus_half", [P, T])
        wr_sb = sb("w_router", [P, E])
        br_row = sb("br_row", [P, E])
        iota8 = sb("iota8", [P, E])
        y1 = sb("y1", [P, IT, D])
        yT = sb("yT", [P, GI])
        lg = sb("logits", [P, IT, E])
        top = sb("top", [P, IT, 8])
        topi = sb("topi", [P, IT, 8], U32)
        lgs = sb("logits_shifted", [P, IT, E])
        chosen = sb("chosen", [P, IT, 2, E])
        picked = sb("picked", [P, IT, 2, E])
        either = sb("either", [P, IT, E], BF16)
        place = sb("place", [P, IT, E])
        carry = sb("carry", [P, E])
        region0 = sb("region_start", [P, E])
        slotf = sb("slot_fp32", [P, IT, 2])
        slot = sb("slot", [P, IT, 2], U32)
        rden = sb("rden", [P, IT])
        held = sb("held_pool", [P, 8])
        hold = sb("hold", [P, 1])
        dest = sb("dest", [P, T, 2])
        pay = sb("payload", [P, IT, 2, PW])
        padt = sb("padding", [P, E + SPARE, PW])
        gcol = sb("ln_g_col", [P, E])
        bcol = sb("ln_b_col", [P, E])
        ntile = sb("tiles_per_expert", [P, 4, E])
        ntile_i = sb("tiles_per_expert_int", [P, 2, E], I32)
        kk = sb("tile_numbers", [P, NT])
        cmp = sb("tile_past_expert", [P, 2, E, NT])
        tab = sb("tile_table", [P, 4, NT])
        table = sb("tile_table_int", [P, 2, NT], I32)
        pad_at = sb("pad_rows", [P, E], I32)
        xs = sb("tile_rows", [P, 4, PW])
        dq = sb("tile_dest", [P, 4], U32)
        gq = sb("tile_gate", [P, 4])
        xT = sb("tile_T", [P, 2, P])
        yb = sb("y_biased", [P, 2, D])
        yo = sb("y_out", [P, 4, D])
        flat = ring[:].rearrange("p a b c -> p (a b c)")
        hb = flat[:, 0:2 * H].rearrange("p (a h) -> p a h", a=2)
        hg = flat[:, 2 * H:4 * H].rearrange("p (a h) -> p a h", a=2)
        hT = flat[:, 4 * H:6 * H].rearrange("p (a h) -> p a h", a=2)
        res = flat.rearrange("p (k t d) -> p k t d", k=2, t=T)

        ps = ctx.enter_context(nc.psum_tensor("psum", [P, 8, 512], FP32))
        SUMS, TURN, Y_T, SMALL = 0, 2, 6, 7
        psH, psT, psX, psY = 0, 2, 4, 5

        ld_small, ld_x, ld_w = sem("ld_small"), [sem("ld_x0"), sem("ld_x1")], sem("ld_w")
        ld_ctx = [sem(f"ld_ctx{k}") for k in range(4)]
        ld_bias = sem("ld_bias")
        adj_ld = [sem(f"adj_loaded{k}") for k in range(RING)]
        consts = sem("consts_ready")
        dve_own, act_own, pool_own, pool_held = sem("dve_own"), sem("act_own"), sem("pool_own"), sem("pool_held")
        folded, folded_sb = sem("folded"), sem("folded_sb")
        ctxT_ps, ctxT_sb, ctxT_used = sem("ctxT_ps"), sem("ctxT_sb"), sem("ctxT_used")
        rowmax, allmax, u_ready, beta_in, beta_ok = (sem(n) for n in ("rowmax", "allmax", "u_ready", "beta_in", "beta_ok"))
        diag_ready, brow_ps = sem("diag_ready"), sem("brow_ps")
        var_ready, rstd_ready = sem("var_ready"), sem("rstd_ready")
        tested, turned, t_ready, masked, p_free = (sem(n) for n in ("adj_tested", "adj_turned", "t_ready", "masked", "p_free"))
        sums_free, sums_saved = sem("sums_free"), sem("sums_saved")
        y_ready, yT_ps, yT_sb, lg_ps, lg_in, lg_exp = (sem(n) for n in ("y_ready", "yT_ps", "yT_sb", "lg_ps", "lg_in", "lg_exp"))
        xn_ready, pay_ready, either_ok, rank_ps, slot_ok, scattered = (sem(n) for n in ("xn_ready", "pay_ready", "either_ok", "rank_ps", "slot_ok", "scattered"))
        lnb_ps, bias_ready, table_ok, pads_out = sem("lnb_ps"), sem("bias_ready"), sem("table_ok"), sem("pads_out")
        xs_ld = [sem(f"rows_loaded{k}") for k in range(4)]
        x_turned, xT_sb = sem("x_turned"), sem("xT_sb")
        h_ps, h_bias, h_gelu, h_turned, hT_sb = (sem(n) for n in ("h_ps", "h_bias", "h_gelu", "h_turned", "hT_sb"))
        y_ps, y_bias, y_gated, row_info = sem("y_ps"), sem("y_bias"), sem("y_gated"), sem("row_info")
        sent = [sem(f"result_sent{k}") for k in range(4)]
        res_ld, summed, stored = [sem(f"results_loaded{k}") for k in range(4)], sem("summed"), sem("stored")

        adj_v = adj.rearrange("(g i p) (c j) -> g c p i j", p=P, i=IT, j=JC)
        out_v = out.rearrange("(t p) d -> p t d", p=P)
        context_v = context.rearrange("(t p) k -> p t k", p=P)
        x_v = x.rearrange("(t p) d -> p t d", p=P)

        def steps(engine, body):
            for q in range(4):
                body(0, q)
            with engine.Fori(1, NT // 4 - 1) as h:
                for q in range(4):
                    body(h, q)
            for q in range(4):
                body(NT // 4 - 1, q)

        def exists(h, q):
            return not (isinstance(h, int) and not 0 <= 4 * h + q < NT)

        block = ctx.enter_context(nc.Block())

        @block.sync
        def _(sp):
            def load(g, c):
                sp.dma_start(ring[:, c % RING], adj_v[g, c]).then_inc(adj_ld[c % RING], 16)

            sp.dma_start(wlr[:, 0:1], w_left.rearrange("(h o) -> h o", o=1)).then_inc(ld_small, 16)
            sp.dma_start(wlr[:, 1:2], w_right.rearrange("(h o) -> h o", o=1)).then_inc(ld_small, 16)
            sp.dma_start(wc_sb[:], W_common).then_inc(ld_small, 16)
            for col, b in ((0, b_left), (1, b_right)):
                sp.dma_start(blr[:, col:col + 1], b.rearrange("(a o) -> a o", a=1).broadcast_to([P, 1])).then_inc(ld_small, 16)
            for k in range(4):
                sp.dma_start(ctx_sb[:, 8 * k:8 * k + 8], context_v[:, 8 * k:8 * k + 8]).then_inc(ld_ctx[k], 16)
            for k in range(2):
                sp.dma_start(xt[:, 16 * k:16 * k + 16], x_v[:, 16 * k:16 * k + 16]).then_inc(ld_x[k], 16)
            for c in range(RING):
                load(0, c)

            def loads(g, last):
                for c in range(C - RING if last else C):
                    sp.wait_ge(tested, g * C + (c + 1))
                    load(g + (1 if c >= C - RING else 0), (c + RING) % C)

            loads(0, False)
            sp.wait_ge(ctxT_ps, T // 2)
            sp.dma_start(w1.rearrange("p (e h) -> p e h", e=E), W1.rearrange("e d h -> d e h")).then_inc(ld_w, 16)
            sp.dma_start(w2.rearrange("p (e k d) -> p e k d", e=E, k=HB), W2.rearrange("e (k p) d -> p e k d", p=P)).then_inc(ld_w, 16)
            with sp.Fori(1, G - 1) as g:
                loads(g, False)
            loads(G - 1, True)

            sp.wait_ge(table_ok, 1)
            sp.dma_start(routed_rows[PADS:PADS + SPARE * P].rearrange("(j p) w -> p j w", p=P), padt[:, E:E + SPARE]).then_inc(pads_out, 16)
            for e in range(E):
                at = sp.value_load(pad_at[0:1, e:e + 1], min_val=e * REGION, max_val=e * REGION + N)
                sp.dma_start(routed_rows[bass.ds(at, P)], padt[:, e]).then_inc(pads_out, 16)
            sp.wait_ge(pads_out, 16 * (E + 1))
            sp.wait_ge(scattered, 16 * 2 * T)

            def rows_in(h, q):
                if not (isinstance(h, int) and h == 0):
                    sp.wait_ge(row_info, 4 * h + (q - 3))
                at = sp.value_load(table[0:1, 1, bass.ds(4 * h + q, 1)], min_val=0, max_val=PADS + (SPARE - 1) * P)
                sp.dma_start(xs[:, q], routed_rows[bass.ds(at, P)]).then_inc(xs_ld[q], 16)

            steps(sp, rows_in)
            for q in range(4):
                sp.wait_ge(sent[q], 16 * (NT // 4))
            for k in range(4):
                for o in range(2):
                    sp.dma_start(res[:, o, 8 * k:8 * k + 8],
                                 results[o * N + k * 8 * P:o * N + (k + 1) * 8 * P].rearrange("(t p) d -> p t d", p=P)).then_inc(res_ld[k], 16)
            for k in range(4):
                sp.wait_ge(summed, k + 1)
                sp.dma_start(out_v[:, 8 * k:8 * k + 8], res[:, 0, 8 * k:8 * k + 8]).then_inc(stored, 16)
            sp.wait_ge(stored, 16 * 4)

        @block.gpsimd
        def _(pool):
            own = Count(pool, pool_own)
            for c, (s, n) in enumerate(((masked, DEEP), (p_free, DEEP), (turned, DEEP * JB), (sums_free, 1))):
                nc.gpsimd.memset(held[:, c + 1:c + 2], 0.0).then_inc(s, n)
            nc.gpsimd.memset(ones[:], 1.0).then_inc(pool_own, 1)
            own.n += 1
            own.mark(nc.gpsimd.memset(onesb[:], 1.0))
            own(nc.gpsimd.memset(padt[:], 0.0))
            for dst, src, op in ((ident, ones, ALU.is_equal), (identb, onesb, ALU.is_equal)):
                nc.gpsimd.affine_select(out=dst[:], in_=src[:], compare_op=op, fill=0.0, base=0,
                                        pattern=[[-1, P]], channel_multiplier=1).then_inc(consts, 1)
            nc.gpsimd.memset(half[:], -0.5).then_inc(consts, 1)
            nc.gpsimd.affine_select(out=before[:], in_=onesb[:], compare_op=ALU.is_gt, fill=0.0, base=0,
                                    pattern=[[1, P]], channel_multiplier=-1).then_inc(consts, 1)
            nc.gpsimd.memset(xh[:, :, D:DA], 1.0).then_inc(consts, 1)
            for t, pattern, base, mult in ((iota8[:], [[1, E]], 0, 0), (region0[:], [[REGION, E]], 0, 0), (carry[:], [[REGION, E]], 0, 0),
                                           (kk[:], [[1, NT]], 0, 0), (padt[:, :, D], [[P, E + SPARE]], 2 * N, 1)):
                nc.gpsimd.iota(t, pattern=pattern, base=base, channel_multiplier=mult,
                               allow_small_or_imprecise_dtypes=True).then_inc(consts, 1)
            nc.gpsimd.iota(dest[:], pattern=[[P, T], [N, 2]], base=0, channel_multiplier=1,
                           allow_small_or_imprecise_dtypes=True).then_inc(consts, 1)
            pool.dma_start(wr_sb[:], Wr).then_inc(ld_bias, 16)
            with nc.allow_non_contiguous_dma(reason="1024 elements each"):
                pool.dma_start(gcol[:], ln_g.rearrange("e d -> d e")).then_inc(ld_bias, 16)
                pool.dma_start(bcol[:], ln_b.rearrange("e d -> d e")).then_inc(ld_bias, 16)
            pool.dma_start(br_row[:], br.rearrange("(a e) -> a e", a=1).broadcast_to([P, E])).then_inc(ld_bias, 16)
            pool.dma_start(b2_row[:], b2.rearrange("(a e) d -> a (e d)", a=1).broadcast_to([P, E * D])).then_inc(ld_bias, 16)
            pool.dma_start(b1_row[:], b1.rearrange("(a e) h -> a (e h)", a=1).broadcast_to([P, E * H])).then_inc(ld_bias, 16)

            pool.wait_ge(rowmax, 1)
            nc.gpsimd.partition_all_reduce(rmax[:, 1:2], rmax[:, 0:1], P, bass.bass_isa.ReduceOp.max).then_inc(allmax, 1)
            pool.wait_ge(consts, 3)

            def diagonal(g):
                nc.gpsimd.tensor_tensor(diag[:], ident[:].unsqueeze(1).broadcast_to([P, IT, P]),
                                        beta[:, bass.ds(IT * g, IT)].unsqueeze(2).broadcast_to([P, IT, P]), ALU.mult).then_inc(diag_ready, 1)

            pool.wait_ge(var_ready, 1)
            nc.gpsimd.tensor_tensor(ms[:, 5, 0:16], ms[:, 4, 0:16], half[:, 0:16], ALU.pow).then_inc(rstd_ready, 1)
            pool.wait_ge(beta_ok, 1)
            diagonal(0)
            pool.wait_ge(var_ready, 2)
            nc.gpsimd.tensor_tensor(ms[:, 5, 16:32], ms[:, 4, 16:32], half[:, 0:16], ALU.pow).then_inc(rstd_ready, 1)

            def carry_wait(done):
                pool.wait_ge(pool_held, done + 1)
                nc.gpsimd.tensor_tensor(held[:, 0:1], held[:, 0:1], held[:, 0:1], ALU.mult).then_inc(pool_held, 1)

            nc.gpsimd.memset(held[:, 0:1], 0.0).then_inc(pool_held, 1)

            def next_diagonal(g):
                pool.wait_ge(brow_ps, g + 1)
                diagonal(g + 1)

            def post(g):
                for k in range(2):
                    pool.wait_ge(var_ready, 2 * g + (k + 3))
                    nc.gpsimd.tensor_tensor(ms[:, 5, 0:IT], ms[:, 4, 0:IT], half[:, 0:IT], ALU.pow).then_inc(rstd_ready, 1)
                pool.wait_ge(xn_ready, g + 1)
                nc.gpsimd.tensor_copy(pay[:, :, :, D], dest[:, bass.ds(IT * g, IT)]).then_inc(pay_ready, 1)
                pool.wait_ge(pay_ready, 2 * g + 2)
                pool.wait_ge(slot_ok, g + 1)
                carry_wait(g)
                for i in range(IT):
                    for k in range(2):
                        pool.indirect_dma_start(out=routed_rows, out_offset=bass.IndirectOffsetOnAxis(ap=slot[:, i, k:k + 1], axis=0),
                                                in_=pay[:, i, k], in_offset=None).then_inc(scattered, 16)
                pool.wait_ge(scattered, 16 * 2 * IT * (g + 1))

            next_diagonal(0)
            with pool.Fori(1, G - 1) as g:
                next_diagonal(g)
                post(g - 1)
            post(G - 2)
            post(G - 1)

            def send(h, q):
                pool.wait_ge(y_gated, 4 * h + (q + 1))
                carry_wait(4 * h + (q + G))
                pool.indirect_dma_start(out=results, out_offset=bass.IndirectOffsetOnAxis(ap=dq[:, q:q + 1], axis=0),
                                        in_=yo[:, q], in_offset=None).then_inc(sent[q], 16)

            steps(pool, send)

        @block.scalar
        def _(act):
            own = Count(act, act_own)
            for n in range(T // 2):
                act.wait_ge(ctxT_ps, n + 1)
                if n >= 2:
                    act.wait_ge(ctxT_used, n - 1)
                nc.scalar.activation(ctxT[:, n % 2], ps[:, 5 + n % 2], ACT.Copy).then_inc(ctxT_sb, 1)
            act.wait_ge(allmax, 2)
            nc.scalar.activation(uv[:, 0], lr[:, 1], ACT.Exp, bias=rmax[:, 2:3]).then_inc(u_ready, 1)
            nc.scalar.activation(uv[:, 1], lr[:, 1], ACT.Exp, bias=rmax[:, 3:4], scale=SLOPE).then_inc(u_ready, 1)
            act.wait_ge(beta_in, 1)
            nc.scalar.activation(beta[:], lR[:], ACT.Exp, scale=SLOPE - 1.0).then_inc(beta_ok, 1)
            act.wait_ge(u_ready, 3)

            def save_sums(g):
                act.wait_ge(p_free, g * NB + (NB + DEEP))
                nc.scalar.activation(gsum[:].rearrange("p (a b) d -> p a (b d)", a=2),
                                     ps[:, SUMS:SUMS + 2, 0:2 * DA], ACT.Copy).then_inc(sums_free, 1)

            def post_T(g):
                act.wait_ge(yT_ps, g + 1)
                nc.scalar.activation(yT[:], ps[:, Y_T], ACT.Copy).then_inc(yT_sb, 1)

            def post_twin(g):
                act.wait_ge(xn_ready, g + 1)
                nc.scalar.activation(pay[:, :, 1, 0:D], pay[:, :, 0, 0:D], ACT.Copy).then_inc(pay_ready, 1)

            def post_exp(g):
                act.wait_ge(lg_in, g + 1)
                nc.scalar.activation(lg[:], lgs[:], ACT.Exp).then_inc(lg_exp, 1)

            def group(g, before_it):
                act.wait_ge(brow_ps, g + 1)
                act.wait_ge(masked, g * NB + DEEP)
                own(nc.scalar.activation(beta_row[:], ps[:, SMALL], ACT.Copy))
                for b in range(NB):
                    if before_it:
                        if b == 2:
                            save_sums(g - 1)
                        if b == POST_T:
                            post_T(g - 1)
                        if b == POST_TWIN:
                            post_twin(g - 1)
                        if b == POST_EXP:
                            post_exp(g - 1)
                    act.wait_ge(masked, g * NB + (b + 1))
                    nc.scalar.activation(tbuf[:, b % DEEP], beta_row[:], ACT.Relu, bias=uv[:, 2, b:b + 1],
                                         scale=uv[:, 1, b:b + 1]).then_inc(t_ready, 1)

            group(0, False)
            with act.Fori(1, G) as g:
                own.enter(g - 1, 1)
                group(g, True)
                own.leave(G - 1)
            save_sums(G - 1)
            post_T(G - 1)
            post_twin(G - 1)
            post_exp(G - 1)

            def turn_out(h, q):
                if not (isinstance(h, int) and 4 * h + q < 2):
                    act.wait_ge(h_ps, 4 * h + (q - 1))
                act.wait_ge(x_turned, 4 * h + (q + 1))
                nc.scalar.activation(xT[:, q % 2], ps[:, psX, 0:P], ACT.Copy).then_inc(xT_sb, 1)

            def gelu(h, q):
                if not (isinstance(h, int) and 4 * h + q < 2):
                    act.wait_ge(h_turned, 4 * h + (q - 1))
                act.wait_ge(h_bias, 4 * h + (q + 1))
                nc.scalar.activation(hg[:, q % 2], hb[:, q % 2], ACT.Gelu).then_inc(h_gelu, 1)

            def gate(h, q):
                if not (isinstance(h, int) and h == 0):
                    act.wait_ge(sent[q % 4], 16 * h)
                act.wait_ge(y_bias, 4 * h + (q + 1))
                nc.scalar.activation(yo[:, q], yb[:, q % 2], ACT.Copy, scale=gq[:, q:q + 1]).then_inc(y_gated, 1)

            turn_out(0, 0)
            turn_out(0, 1)
            gelu(0, 0)

            def step(h, q):
                if exists(h, q + 2):
                    turn_out(h + (q + 2) // 4, (q + 2) % 4)
                if exists(h, q + 1):
                    gelu(h + (q + 1) // 4, (q + 1) % 4)
                if exists(h, q - 1):
                    gate(h - (1 if q == 0 else 0), (q - 1) % 4)

            steps(act, step)
            gate(NT // 4 - 1, 3)

        @block.vector
        def _(dve):
            own = Count(dve, dve_own)

            def centre(a, n):
                v = [stats[:, a:a + n, k] for k in range(6)]
                m = [ms[:, k, a:a + n] for k in range(6)]
                own.mark(nc.vector.tensor_tensor(m[0], v[1], v[4], ALU.add))
                own.mark(nc.vector.tensor_tensor(m[1], v[1], v[4], ALU.subtract))
                own(nc.vector.tensor_tensor(m[2], v[2], v[5], ALU.add))
                own.mark(nc.vector.tensor_scalar(m[3], m[0], 0.5, None, ALU.mult))
                own(nc.vector.tensor_tensor(m[5], m[1], m[1], ALU.mult))
                own(nc.vector.scalar_tensor_tensor(m[0], m[5], D / 4.0, m[2], ALU.mult, ALU.add))
                nc.vector.tensor_scalar(m[4], m[0], 1.0 / D, EPS, ALU.mult, ALU.add).then_inc(var_ready, 1)

            dve.wait_ge(folded, 1)
            nc.vector.tensor_copy(wck[:].rearrange("p k o -> p (k o)"), ps[:, 1, 0:2 * KC]).then_inc(folded_sb, 1)
            def stats_of(k):
                dve.wait_ge(ld_x[k], 16)
                for t in range(16 * k, 16 * k + 16):
                    own.mark(nc.vector.bn_stats(stats[:, t], xt[:, t]))
                own.wait()
                centre(16 * k, 16)

            def normal(k):
                dve.wait_ge(rstd_ready, k + 1)
                for t in range(16 * k, 16 * k + 16):
                    own.mark(nc.vector.tensor_scalar(xh[:, t, 0:D], xt[:, t], ms[:, 3, t:t + 1], ms[:, 5, t:t + 1],
                                                     ALU.subtract, ALU.mult))

            stats_of(0)
            dve.wait_ge(ctxT_used, T // 2)
            dve.wait_ge(ld_small, 5 * 16)
            for o in (1, 0):
                own.mark(nc.vector.tensor_scalar(lr[:, o], ps[:, 0, 0:2 * T].rearrange("p (t o) -> p o t", o=2)[:, o],
                                                 blr[:, o:o + 1], None, ALU.add))
            own.wait()
            nc.vector.tensor_reduce(rmax[:, 0:1], lr[:, 1], AX_X, ALU.max).then_inc(rowmax, 1)
            dve.wait_ge(allmax, 1)
            own.mark(nc.vector.tensor_scalar(rmax[:, 2:3], rmax[:, 1:2], -1.0, None, ALU.mult))
            nc.vector.tensor_scalar(rmax[:, 3:4], rmax[:, 1:2], -SLOPE, None, ALU.mult).then_inc(allmax, 1)
            nc.vector.tensor_scalar(lR[:], lr[:, 0], rmax[:, 1:2], 0.0, ALU.add, ALU.max).then_inc(beta_in, 1)
            dve.wait_ge(u_ready, 1)
            nc.vector.tensor_scalar(uv[:, 2], uv[:, 0], -1.0, None, ALU.mult).then_inc(u_ready, 1)

            def test(g, c):
                dve.wait_ge(adj_ld[c % RING], 16 * (g * (C // RING) + (c // RING + 1)))
                dve.wait_ge(turned, g * NB + (c + 1) * JB)
                nc.vector.tensor_scalar(mring[:, c % RING], ring[:, c % RING], 0.0, None, ALU.is_gt).then_inc(tested, 1)

            test(0, 0)
            normal(0)
            stats_of(1)
            normal(1)
            own.wait()

            def post_residual(g):
                rows = bass.ds(IT * g, IT)
                dve.wait_ge(sums_free, g + 2)
                own(nc.vector.reciprocal(rden[:], gsum[:, :, D]))
                own(nc.vector.tensor_tensor(y1[:], gsum[:, :, 0:D], rden[:].unsqueeze(2).broadcast_to([P, IT, D]), ALU.mult))
                own(nc.vector.scalar_tensor_tensor(xt[:, rows], y1[:], 0.0, xt[:, rows], ALU.max, ALU.add))
                nc.vector.memset(hold[:], 0.0)
                for i in range(IT):
                    own.mark(nc.vector.bn_stats(stats[:, i], xt[:, IT * g + i]))
                own.wait()
                centre(0, IT)

            def post_norm(g):
                dve.wait_ge(rstd_ready, 2 * g + 3)
                for i in range(IT):
                    own.mark(nc.vector.tensor_scalar(y1[:, i], xt[:, IT * g + i], ms[:, 3, i:i + 1], ms[:, 5, i:i + 1],
                                                     ALU.subtract, ALU.mult))
                own.wait()
                nc.vector.memset(hold[:], 0.0).then_inc(y_ready, 1)
                for i in range(IT):
                    own.mark(nc.vector.bn_stats(stats[:, i], y1[:, i]))
                own.wait()
                centre(0, IT)

            def post_tokens(g):
                dve.wait_ge(rstd_ready, 2 * g + 4)
                for i in range(IT):
                    own.mark(nc.vector.tensor_scalar(pay[:, i, 0, 0:D], y1[:, i], ms[:, 3, i:i + 1], ms[:, 5, i:i + 1],
                                                     ALU.subtract, ALU.mult))
                own.wait()
                nc.vector.memset(hold[:], 0.0).then_inc(xn_ready, 1)

            def post_logits(g):
                dve.wait_ge(lg_ps, g + 1)
                own(nc.vector.tensor_tensor(lg[:], ps[:, SMALL, 0:IT * E].rearrange("p (i e) -> p i e", i=IT),
                                            br_row[:].unsqueeze(1).broadcast_to([P, IT, E]), ALU.add))
                own(nc.vector.tensor_reduce(rden[:], lg[:], AX_X, ALU.max))
                nc.vector.tensor_tensor(lgs[:], lg[:], rden[:].unsqueeze(2).broadcast_to([P, IT, E]), ALU.subtract).then_inc(lg_in, 1)

            def post_top(g):
                dve.wait_ge(lg_exp, g + 1)
                nc.vector.memset(hold[:], 0.0)
                for i in range(IT):
                    own.mark(nc.vector.max(top[:, i], lg[:, i]))
                own.wait()
                nc.vector.memset(hold[:], 0.0)
                for i in range(IT):
                    own.mark(nc.vector.max_index(topi[:, i], top[:, i], lg[:, i]))
                own(nc.vector.tensor_tensor(rden[:], top[:, :, 0], top[:, :, 1], ALU.add))
                own.mark(nc.vector.reciprocal(rden[:], rden[:]))
                own(nc.vector.tensor_tensor(chosen[:], iota8[:].unsqueeze(1).unsqueeze(1).broadcast_to([P, IT, 2, E]),
                                            topi[:, :, 0:2].unsqueeze(3).broadcast_to([P, IT, 2, E]), ALU.is_equal))
                nc.vector.tensor_tensor(either[:], chosen[:, :, 0], chosen[:, :, 1], ALU.add).then_inc(either_ok, 1)
                own.mark(nc.vector.tensor_tensor(pay[:, :, :, D + 1], top[:, :, 0:2],
                                                 rden[:].unsqueeze(2).broadcast_to([P, IT, 2]), ALU.mult))

            def post_slots(g):
                dve.wait_ge(rank_ps, g + 1)
                own(nc.vector.tensor_tensor(place[:], ps[:, SMALL, 64:64 + IT * E].rearrange("p (i e) -> p i e", i=IT),
                                            carry[:].unsqueeze(1).broadcast_to([P, IT, E]), ALU.add))
                own.mark(nc.vector.tensor_tensor(carry[:], carry[:], ps[:, SMALL, 64 + IT * E:64 + IT * E + E], ALU.add))
                own(nc.vector.tensor_tensor(picked[:], chosen[:], place[:].unsqueeze(2).broadcast_to([P, IT, 2, E]), ALU.mult))
                own(nc.vector.tensor_reduce(slotf[:], picked[:], AX_X, ALU.add))
                nc.vector.tensor_copy(slot[:], slotf[:]).then_inc(slot_ok, 1)

            def group(g, first, last):
                for b in range(NB):
                    if b % JB == 0 and not (last and b == NB - JB):
                        test(g + (1 if b == NB - JB else 0), (b // JB + 1) % C)
                    if not first:
                        if b == 4:
                            post_residual(g - 1)
                        if b == 6:
                            post_norm(g - 1)
                        if b == 9:
                            post_tokens(g - 1)
                        if b == 13:
                            post_logits(g - 1)
                        if b == 17:
                            post_top(g - 1)
                        if b == 23:
                            post_slots(g - 1)
                    dve.wait_ge(turned, g * NB + (b + 1 + DEEP * JB))
                    dve.wait_ge(t_ready, g * NB + (b + 1))
                    dve.wait_ge(p_free, g * NB + (b + 1))
                    nc.vector.scalar_tensor_tensor(pbuf[:, b % DEEP], tbuf[:, b % DEEP], uv[:, 0, b:b + 1],
                                                   ps[:, TURN + b % DEEP].bitcast(BF16)[:, 0:GI],
                                                   ALU.add, ALU.mult).then_inc(masked, 1)

            dve.wait_ge(ld_bias, 6 * 16)
            dve.wait_ge(consts, 11)
            group(0, True, False)
            with dve.Fori(1, G - 1) as g:
                own.enter(g - 1, POST_OWN)
                group(g, False, False)
                own.leave(G - 2)
            group(G - 1, False, True)
            post_residual(G - 1)
            post_norm(G - 1)
            post_tokens(G - 1)
            post_logits(G - 1)
            post_top(G - 1)
            post_slots(G - 1)

            own.wait()
            own(nc.vector.tensor_tensor(ntile[:, 0], carry[:], region0[:], ALU.subtract))
            own(nc.vector.tensor_scalar(ntile_i[:, 0], ntile[:, 0], float(P - 1), None, ALU.add))
            own.mark(nc.vector.tensor_copy(pad_at[:], carry[:]))
            own(nc.vector.tensor_scalar(ntile_i[:, 1], ntile_i[:, 0], P.bit_length() - 1, None, ALU.logical_shift_right))
            own(nc.vector.tensor_copy(ntile[:, 1], ntile_i[:, 1]))
            own.mark(nc.vector.tensor_scalar(ntile[:, 2], ntile[:, 1], -float(P), float(REGION), ALU.mult, ALU.add))
            own(nc.vector.tensor_copy(ntile[:, 3, 0:1], ntile[:, 1, 0:1]))
            for e in range(1, E):
                own(nc.vector.tensor_tensor(ntile[:, 3, e:e + 1], ntile[:, 3, e - 1:e], ntile[:, 1, e:e + 1], ALU.add))
            wideband = [P, E, NT]
            own(nc.vector.tensor_tensor(cmp[:, 0], kk[:].unsqueeze(1).broadcast_to(wideband),
                                        ntile[:, 3].unsqueeze(2).broadcast_to(wideband), ALU.is_ge))
            own(nc.vector.tensor_tensor(cmp[:, 1], cmp[:, 0], ntile[:, 2].unsqueeze(2).broadcast_to(wideband), ALU.mult))
            for k in range(2):
                own.mark(nc.vector.tensor_reduce(tab[:, k], cmp[:, k].rearrange("p e n -> p n e"), AX_X, ALU.add))
            own.wait()
            own.mark(nc.vector.scalar_tensor_tensor(tab[:, 2], kk[:], float(P), tab[:, 1], ALU.mult, ALU.add))
            own(nc.vector.tensor_scalar(table[:, 0], tab[:, 0], float(E - 1), None, ALU.min))
            nc.vector.tensor_copy(table[:, 1], tab[:, 2]).then_inc(table_ok, 1)

            for e in range(E):
                dve.wait_ge(lnb_ps, e + 1)
                at = slice(e * H, (e + 1) * H)
                own(nc.vector.tensor_tensor(b1_row[:, at], ps[:, 2 + e % 2], b1_row[:, at], ALU.add))
                nc.vector.tensor_scalar(w1[:, at], w1[:, at], gcol[:, e:e + 1], None, ALU.mult).then_inc(bias_ready, 1)

            def bias_h(h, q):
                e = dve.value_load(table[0:1, 0, bass.ds(4 * h + q, 1)], min_val=0, max_val=E - 1)
                if not (isinstance(h, int) and 4 * h + q < 2):
                    dve.wait_ge(h_gelu, 4 * h + (q - 1))
                dve.wait_ge(h_ps, 4 * h + (q + 1))
                nc.vector.tensor_tensor(hb[:, q % 2], ps[:, psH + q % 2], b1_row[:, bass.ds(e * H, H)], ALU.add).then_inc(h_bias, 1)

            def turn_out(h, q):
                if not (isinstance(h, int) and 4 * h + q < 2):
                    dve.wait_ge(y_ps, 4 * h + (q - 1))
                dve.wait_ge(h_turned, 4 * h + (q + 1))
                nc.vector.tensor_copy(hT[:, q % 2], ps[:, psT + q % 2]).then_inc(hT_sb, 1)

            def info(h, q):
                if not (isinstance(h, int) and h == 0):
                    dve.wait_ge(sent[q], 16 * h)
                nc.vector.tensor_copy(dq[:, q:q + 1], xs[:, q, D:D + 1])
                nc.vector.tensor_copy(gq[:, q:q + 1], xs[:, q, D + 1:D + 2]).then_inc(row_info, 1)

            def bias_y(h, q):
                e = dve.value_load(table[0:1, 0, bass.ds(4 * h + q, 1)], min_val=0, max_val=E - 1)
                if not (isinstance(h, int) and 4 * h + q < 2):
                    dve.wait_ge(y_gated, 4 * h + (q - 1))
                dve.wait_ge(y_ps, 4 * h + (q + 1))
                nc.vector.tensor_tensor(yb[:, q % 2], ps[:, psY + q % 2, 0:D], b2_row[:, bass.ds(e * D, D)], ALU.add).then_inc(y_bias, 1)

            bias_h(0, 0)

            def step(h, q):
                if exists(h, q + 1):
                    bias_h(h + (q + 1) // 4, (q + 1) % 4)
                turn_out(h, q)
                info(h, q)
                if exists(h, q - 1):
                    bias_y(h - (1 if q == 0 else 0), (q - 1) % 4)

            steps(dve, step)
            bias_y(NT // 4 - 1, 3)

            for k in range(4):
                at = slice(8 * k, 8 * k + 8)
                dve.wait_ge(res_ld[k], 32)
                own(nc.vector.tensor_tensor(res[:, 0, at], res[:, 0, at], res[:, 1, at], ALU.add))
                nc.vector.tensor_tensor(res[:, 0, at], res[:, 0, at], xt[:, at], ALU.add).then_inc(summed, 1)

        @block.tensor
        def _(pe):
            pe.wait_ge(ld_small, 5 * 16)
            for k in range(KC):
                last = nc.tensor.matmul(ps[:, 1, 2 * k:2 * k + 2], wc_sb[:, k * P:(k + 1) * P], wlr[:], start=True, stop=True)
            last.then_inc(folded, 1)
            pe.wait_ge(folded_sb, 1)
            pe.wait_ge(consts, 2)

            def context_dot(n):
                pe.wait_ge(ctxT_sb, n + 1)
                for i in range(2):
                    for k in range(KC):
                        last = nc.tensor.matmul(ps[:, 0, 2 * (2 * n + i):2 * (2 * n + i) + 2],
                                                ctxT[:, n % 2, (2 * i + k) * P:(2 * i + k + 1) * P], wck[:, k],
                                                start=(k == 0), stop=(k == KC - 1))
                last.then_inc(ctxT_used, 1)

            for n in range(T // 2):
                if n % 4 == 0:
                    pe.wait_ge(ld_ctx[n // 4], 16)
                if n >= 2:
                    pe.wait_ge(ctxT_sb, n - 1)
                for i in range(2):
                    for k in range(KC):
                        last = nc.tensor.transpose(ps[:, 5 + n % 2, (2 * i + k) * P:(2 * i + k + 1) * P],
                                                   ctx_sb[:, 2 * n + i, k * P:(k + 1) * P], ident[:])
                last.then_inc(ctxT_ps, 1)
                if n:
                    context_dot(n - 1)
            context_dot(T // 2 - 1)

            def beta_rows(g):
                pe.wait_ge(diag_ready, g + 1)
                nc.tensor.matmul(ps[:, SMALL], ones[:], diag[:].rearrange("p a b -> p (a b)"), start=True, stop=True).then_inc(brow_ps, 1)

            def turn(g, b):
                c = b // JB
                if b % JB == 0:
                    pe.wait_ge(tested, g * C + (c + 1))
                pe.wait_ge(masked, g * NB + (b + 1))
                for i in range(IT):
                    last = nc.tensor.transpose(ps[:, TURN + b % DEEP].bitcast(BF16)[:, i * P:(i + 1) * P],
                                               mring[:, c % RING, i, (b % JB) * P:(b % JB + 1) * P], identb[:])
                last.then_inc(turned, 1)

            def add_up(g, b):
                pe.wait_ge(masked, g * NB + (b + 1 + DEEP))
                if b == 0:
                    pe.wait_ge(sums_free, g + 1)
                for i in range(IT):
                    at = ps[:, SUMS + i // 2, (i % 2) * DA:(i % 2 + 1) * DA]
                    last = nc.tensor.matmul(at, pbuf[:, b % DEEP, i * P:(i + 1) * P], xh[:, b],
                                            start=(b == 0 and i % 2 == 0), stop=(b == NB - 1), skip_group_check=True)
                last.then_inc(p_free, 1)

            def post_T(g):
                pe.wait_ge(y_ready, g + 1)
                for i in range(IT):
                    last = nc.tensor.transpose(ps[:, Y_T, i * P:(i + 1) * P], y1[:, i], ident[:])
                last.then_inc(yT_ps, 1)

            def post_logits(g):
                pe.wait_ge(yT_sb, g + 1)
                for i in range(IT):
                    last = nc.tensor.matmul(ps[:, SMALL, i * E:(i + 1) * E], yT[:, i * P:(i + 1) * P], wr_sb[:], start=True, stop=True)
                last.then_inc(lg_ps, 1)

            def post_ranks(g):
                pe.wait_ge(either_ok, g + 1)
                for i in range(IT + 1):
                    at = ps[:, SMALL, 64 + i * E:64 + (i + 1) * E]
                    parts = [(onesb, j) for j in range(i)] + ([(before, i)] if i < IT else [])
                    for n, (m, j) in enumerate(parts):
                        last = nc.tensor.matmul(at, m[:], either[:, j], start=(n == 0), stop=(n == len(parts) - 1))
                last.then_inc(rank_ps, 1)

            def group(g, first, last):
                for b in range(NB):
                    if not (last and b + 2 >= NB):
                        turn(g + (1 if b + 2 >= NB else 0), (b + 2) % NB)
                    add_up(g, b)
                    if not first:
                        if b == 8:
                            post_T(g - 1)
                        if b == 11:
                            post_logits(g - 1)
                        if b == 20:
                            post_ranks(g - 1)
                    if b == 28 and not last:
                        beta_rows(g + 1)

            beta_rows(0)
            turn(0, 0)
            turn(0, 1)
            group(0, True, False)
            with pe.Fori(1, G - 1) as g:
                group(g, False, False)
            group(G - 1, False, True)
            pe.wait_ge(ld_w, 32)

            def fold(e):
                if e >= 2:
                    pe.wait_ge(bias_ready, e - 1)
                nc.tensor.matmul(ps[:, 2 + e % 2], bcol[:, e:e + 1].broadcast_to([P, P]), w1[:, e * H:(e + 1) * H],
                                 start=True, stop=True).then_inc(lnb_ps, 1)

            fold(0)
            fold(1)
            post_T(G - 1)
            post_logits(G - 1)
            post_ranks(G - 1)
            for e in range(2, E):
                fold(e)

            def rows_T(h, q):
                pe.wait_ge(xs_ld[q], 16 * h + 16)
                if not (isinstance(h, int) and 4 * h + q < 1):
                    pe.wait_ge(xT_sb, 4 * h + q)
                nc.tensor.transpose(ps[:, psX, 0:P], xs[:, q, 0:D], ident[:]).then_inc(x_turned, 1)

            def up(h, q):
                e = pe.value_load(table[0:1, 0, bass.ds(4 * h + q, 1)], min_val=0, max_val=E - 1)
                pe.wait_ge(xT_sb, 4 * h + (q + 1))
                if not (isinstance(h, int) and 4 * h + q < 2):
                    pe.wait_ge(h_bias, 4 * h + (q - 1))
                nc.tensor.matmul(ps[:, psH + q % 2], xT[:, q % 2], w1[:, bass.ds(e * H, H)], start=True, stop=True).then_inc(h_ps, 1)

            def hidden_T(h, q):
                pe.wait_ge(h_gelu, 4 * h + (q + 1))
                if not (isinstance(h, int) and 4 * h + q < 2):
                    pe.wait_ge(hT_sb, 4 * h + (q - 1))
                for j in range(HB):
                    last = nc.tensor.transpose(ps[:, psT + q % 2, j * P:(j + 1) * P], hg[:, q % 2, j * P:(j + 1) * P], ident[:])
                last.then_inc(h_turned, 1)

            def down(h, q):
                e = pe.value_load(table[0:1, 0, bass.ds(4 * h + q, 1)], min_val=0, max_val=E - 1)
                pe.wait_ge(hT_sb, 4 * h + (q + 1))
                if not (isinstance(h, int) and 4 * h + q < 2):
                    pe.wait_ge(y_bias, 4 * h + (q - 1))
                for j in range(HB):
                    last = nc.tensor.matmul(ps[:, psY + q % 2, 0:D], hT[:, q % 2, j * P:(j + 1) * P],
                                            w2[:, bass.ds(e * H + j * D, D)], start=(j == 0), stop=(j == HB - 1))
                last.then_inc(y_ps, 1)

            pe.wait_ge(bias_ready, E)
            pe.wait_ge(table_ok, 1)
            rows_T(0, 0)
            rows_T(0, 1)
            up(0, 0)

            def step(h, q):
                if exists(h, q + 2):
                    rows_T(h + (q + 2) // 4, (q + 2) % 4)
                if exists(h, q + 1):
                    up(h + (q + 1) // 4, (q + 1) % 4)
                hidden_T(h, q)
                if exists(h, q - 1):
                    down(h - (1 if q == 0 else 0), (q - 1) % 4)

            steps(pe, step)
            down(NT // 4 - 1, 3)


_INS = ['x', 'adj', 'L0_gnn_context', 'L0_gnn_W_common', 'L0_gnn_w_left', 'L0_gnn_b_left', 'L0_gnn_w_right',
        'L0_gnn_b_right', 'L0_ffn_Wr', 'L0_ffn_br', 'L0_ffn_ln_g', 'L0_ffn_ln_b', 'L0_ffn_W1', 'L0_ffn_b1',
        'L0_ffn_W2', 'L0_ffn_b2']


def kernel(**inputs):
    import numpy as np
    import concourse.bacc as bacc
    from concourse.bass_utils import run_bass_kernel_spmd

    nc = bacc.Bacc("TRN2", target_bir_lowering=False, num_devices=1)
    arrays, args = {}, []
    for name in _INS:
        a = np.ascontiguousarray(inputs[name])
        if a.ndim == 0:
            a = a.reshape(1)
        arrays[f"in_{name}"] = a
        args.append(nc.dram_tensor(f"in_{name}", a.shape, mybir.dt.from_np(a.dtype), kind="ExternalInput").ap())
    args.append(nc.dram_tensor("out", (N, D), FP32, kind="ExternalOutput").ap())
    build(nc, *args)
    r = run_bass_kernel_spmd(nc, [arrays], core_ids=[0])
    return r.results[0]["out"]
```

```python
import concourse.bass as bass
from concourse import mybir
from contextlib import ExitStack

FP32 = mybir.dt.float32
FP32R = mybir.dt.float32r
U32 = mybir.dt.uint32
ALU = mybir.AluOpType
BF16 = mybir.dt.bfloat16
I32 = mybir.dt.int32
ACT = mybir.ActivationFunctionType
AX_X = mybir.AxisListType.X

P = 128
N = 4096
D = 128
T = N // P
KC = 256 // P
IT = 4
G = T // IT
GI = IT * P
JC = 512
C = N // JC
JB = JC // P
RING = 4
NB = N // P
E = 8
H = 512
HB = H // P
DA = D + 1
SLOPE = 0.2
EPS = 1e-5
CT = 4
PAIRS = 7
XT = 8
DEEP = 4
AHEAD = 2
POST_OWN = 26
ACT_OWN = 2
POOL_OWN = 19
PW = D + 2
TR = 2 * P
REGION = N + TR
NT = 2 * N // TR + E - 1
EARLY = 16
UNROLL = 8
LAST = (NT - 1) // UNROLL
XS = 4
PADS = E * REGION
SPARE = NT - 2 * N // TR


class Count:

    def __init__(self, engine, sem):
        self.engine, self.sem, self.base, self.n = engine, sem, 0, 0

    def __call__(self, instruction):
        instruction.then_inc(self.sem, 1)
        self.n += 1
        self.wait()

    def mark(self, instruction):
        instruction.then_inc(self.sem, 1)
        self.n += 1

    def wait(self, but=0):
        self.engine.wait_ge(self.sem, self.base + self.n - but)

    def enter(self, i, per_step):
        self.outside, self.per_step = self.base + self.n, per_step
        self.base, self.n = self.outside + i * per_step, 0

    def leave(self, steps):
        assert self.n == self.per_step, (self.n, self.per_step)
        self.base, self.n = self.outside + steps * self.per_step, 0


def build(nc, x, adj, context, W_common, w_left, b_left, w_right, b_right,
          Wr, br, ln_g, ln_b, W1, b1, W2, b2, out):
    ctx = ExitStack()
    with ctx:
        def sb(name, shape, dt=FP32):
            return ctx.enter_context(nc.sbuf_tensor(name, shape, dt))

        def sem(name):
            return ctx.enter_context(nc.semaphore(name))

        routed_rows = nc.dram_tensor("routed_rows", (PADS + SPARE * TR, PW), FP32, kind="Internal").ap()
        results = nc.dram_tensor("results", (2 * N + (E + SPARE) * TR, D), FP32, kind="Internal").ap()

        mring = sb("mask_ring", [P, RING, IT, JC], BF16)
        xt = sb("x_rows", [P, T, D])
        xh_all = sb("x_norm_aug", [P, T, DA + 1])
        xh = xh_all[:, :, 0:DA]
        beta_row = sb("beta_row", [P, GI])
        wide = sb("wide", [P, 2 * E * H])
        ctx_sb = wide[:, :].rearrange("p (t k) -> p t k", t=T)
        w1 = wide[:, 0:E * H]
        w2 = wide[:, E * H:2 * E * H]
        b1c = sb("b1_columns", [P, E * HB])
        b2_row = sb("b2_row", [P, E * D])
        tbuf = sb("t_buf", [P, DEEP, GI])
        pbuf = sb("p_buf", [P, DEEP, GI])
        gsum = sb("graph_sums", [P, IT, DA])
        ident = sb("ident", [P, P])
        identb = sb("ident_bf16", [P, P], BF16)
        ones = sb("ones", [P, P])
        onesb = sb("ones_bf16", [P, P], BF16)
        before = sb("before", [P, P], BF16)
        diag = sb("diag", [P, IT, P])
        wc_sb = sb("w_common", [P, KC * P])
        wlr = sb("w_left_right", [P, 2])
        wck = sb("w_folded", [P, KC, 2])
        wrows = sb("w_folded_rows", [P, 2, KC * P])
        junk = sb("products", [P, 2, KC * P])
        blr = sb("b_left_right", [P, 2])
        ctxT = sb("context_T", [P, 2, IT * P])
        lr = sb("left_right", [P, 2, T])
        rmax = sb("r_max", [P, 4])
        uv = sb("u_v_minus_u", [P, 3, T])
        lR = sb("left_plus_R", [P, T])
        beta = sb("beta", [P, T])
        stats = sb("stats", [P, T, 6])
        ms = sb("mean_scratch", [P, 8, T])
        half = sb("minus_half", [P, T])
        quarter_d, inverse_d, eps = (sb(n, [P, XT]) for n in ("quarter_d", "inverse_d", "eps"))
        wr_sb = sb("w_router", [P, E])
        br_row = sb("br_row", [P, E])
        iota8 = sb("iota8", [P, E])
        post_stats = sb("post_stats", [P, 2, IT, 6])
        pm = sb("post_mean_scratch", [P, 2, 8, IT])
        y1 = sb("y1", [P, IT, D])
        yT = sb("yT", [P, GI])
        lg = sb("logits", [P, IT, E])
        top = sb("top", [P, IT, 8])
        topi = sb("topi", [P, IT, 8], U32)
        lgs = sb("logits_shifted", [P, IT, E])
        chosen = sb("chosen", [P, IT, 2, E])
        picked = sb("picked", [P, IT, 2, E])
        either = sb("either", [P, IT, E], BF16)
        place = sb("place", [P, IT, E])
        carry = sb("carry", [P, E])
        region0 = sb("region_start", [P, E])
        slotf = sb("slot_fp32", [P, IT, 2])
        slot = sb("slot", [P, IT, 2], U32)
        rden = sb("rden", [P, IT])
        rtop = sb("top_scratch", [P, IT])
        held = sb("held_pool", [P, 8])
        hold = sb("hold", [P, 1])
        dest = sb("dest", [P, T, 2])
        pay = sb("payload", [P, IT, 2, PW])
        padt = sb("padding", [P, 2 * E, PW])
        gcol = sb("ln_g_col", [P, E])
        bcol = sb("ln_b_col", [P, E])
        ntile = sb("tiles_per_expert", [P, 4, E])
        ntile_i = sb("tiles_per_expert_int", [P, 2, E], I32)
        kk = sb("tile_numbers", [P, NT])
        cmp = sb("tile_past_expert", [P, 2, E, NT])
        tab = sb("tile_table", [P, 4, NT])
        table = sb("tile_table_int", [P, 2, NT], I32)
        pad_at = sb("pad_rows", [P, E], I32)
        dq = sb("tile_dest", [P, UNROLL, 2], U32)
        gq = sb("tile_gate", [P, UNROLL, 2])
        yo = sb("y_out", [P, UNROLL, 2, D])
        w1_hi = sb("w1_high", [P, E * H])
        taken = sb("tiles_taken_early", [P, 3, E + 1])
        with ExitStack() as graph_layer:
            ring = graph_layer.enter_context(nc.sbuf_tensor("adj_ring", [P, RING, IT, JC], FP32))
        w1e = sb("w1_of_tile", [P, 2, 2, H], FP32R)
        hT = sb("hidden_T", [P, 2, HB, TR])
        xs = sb("tile_rows", [P, XS, 2, PW])
        yb = sb("y_biased", [P, 2, 2, D])
        xT_hi = sb("tile_T_high", [P, 2, TR], FP32R)
        xT_lo = sb("tile_T_low", [P, 2, TR], FP32R)
        sb("rest_of_ring", [P, RING * IT * JC - 2 * 2 * H - 2 * HB * TR - XS * 2 * PW - 2 * 2 * TR - 2 * 2 * D])
        res = ring[:].rearrange("p a b c -> p (a b c)").rearrange("p (k t d) -> p k t d", k=2, t=T)

        ps = ctx.enter_context(nc.psum_tensor("psum", [P, 8, 512], FP32))
        SUMS, TURN, Y_T, BETA = 0, 2, 6, 7
        psH, psX, psY = 0, 4, (5, 7)

        ld_small, ld_x, ld_w = sem("ld_small"), [sem(f"ld_x{k}") for k in range(T // XT)], sem("ld_w")
        ld_ctx = [sem(f"ld_ctx{k}") for k in range(T // CT)]
        ld_bias = sem("ld_bias")
        adj_ld = [sem(f"adj_loaded{k}") for k in range(RING)]
        consts, rows_sb, dots = sem("consts_ready"), sem("folded_rows_sb"), sem("dots")
        dve_own, act_own, pool_own, pool_held = sem("dve_own"), sem("act_own"), sem("pool_own"), sem("pool_held")
        folded, folded_sb = sem("folded"), sem("folded_sb")
        ctxT_ps, ctxT_sb, ctxT_used = sem("ctxT_ps"), sem("ctxT_sb"), sem("ctxT_used")
        rowmax, allmax, u_ready, beta_in, beta_ok = (sem(n) for n in ("rowmax", "allmax", "u_ready", "beta_in", "beta_ok"))
        diag_ready, brow_ps = sem("diag_ready"), sem("brow_ps")
        var_ready, rstd_ready = sem("var_ready"), sem("rstd_ready")
        tested, turned, t_ready, masked, p_free = (sem(n) for n in ("adj_tested", "adj_turned", "t_ready", "masked", "p_free"))
        sums_free, first_sums = sem("sums_free"), sem("first_sums_done")
        y_ready, yT_ps, yT_sb, lg_ps, lg_in, lg_exp = (sem(n) for n in ("y_ready", "yT_ps", "yT_sb", "lg_ps", "lg_in", "lg_exp"))
        rden_ok, relu_ok, x_new, stats_ok, norm_ok = (sem(n) for n in ("rden_ok", "relu_ok", "x_new", "stats_ok", "norm_ok"))
        xn_ready, pay_ready, either_ok, rank_ps, slot_ok, scattered = (sem(n) for n in ("xn_ready", "pay_ready", "either_ok", "rank_ps", "slot_ok", "scattered"))
        lnb_ps, bias_ready, table_ok, pads_out = sem("lnb_ps"), sem("bias_ready"), sem("table_ok"), sem("pads_out")
        xs_ld = [sem(f"rows_loaded{k}") for k in range(XS)]
        x_turned, xT_sb = sem("x_turned"), sem("xT_sb")
        w1_high, w1_split, x_low = sem("w1_high"), sem("w1_split"), sem("x_low")
        w1_there, last_var, last_bias = sem("w1_there"), sem("last_var"), sem("last_bias")
        w1_scaled, pads_known = sem("w1_scaled"), sem("pads_known")
        early_out = sem("early_rows_out")
        x_stats, x_norm_ok, xh_ok = sem("x_stats"), sem("x_norm_ok"), sem("xh_ok")
        h_ps, h_gelu, spares_set, spares_out = sem("h_ps"), sem("h_gelu"), sem("spares_set"), sem("spares_out")
        y_ps, y_added, y_gated, row_info = sem("y_ps"), sem("y_added"), sem("y_gated"), sem("row_info")
        sent = [sem(f"result_sent{k}") for k in range(UNROLL)]
        res_ld, summed, stored = [sem(f"results_loaded{k}") for k in range(4)], sem("summed"), sem("stored")

        adj_v = adj.rearrange("(g i p) (c j) -> g c p i j", p=P, i=IT, j=JC)
        out_v = out.rearrange("(t p) d -> p t d", p=P)
        context_v = context.rearrange("(t p) k -> p t k", p=P)
        x_v = x.rearrange("(t p) d -> p t d", p=P)

        def steps(engine, body, before):
            for k in range(EARLY):
                for serve in before.get(k, ()):
                    serve()
                body(k // UNROLL, k % UNROLL)
            for serve in before.get(EARLY, ()):
                serve()
            with engine.Fori(EARLY // UNROLL, LAST) as h:
                for q in range(UNROLL):
                    body(h, q)
            for q in range(NT - UNROLL * LAST):
                body(LAST, q)

        def shifted(h, q, d):
            return h + (q + d) // UNROLL, (q + d) % UNROLL

        def exists(h, q):
            return not (isinstance(h, int) and not 0 <= UNROLL * h + q < NT)

        block = ctx.enter_context(nc.Block())

        @block.sync
        def _(sp):
            def load(g, c):
                sp.dma_start(ring[:, c % RING], adj_v[g, c]).then_inc(adj_ld[c % RING], 16)

            sp.dma_start(wlr[:, 0:1], w_left.rearrange("(h o) -> h o", o=1)).then_inc(ld_small, 16)
            sp.dma_start(wlr[:, 1:2], w_right.rearrange("(h o) -> h o", o=1)).then_inc(ld_small, 16)
            sp.dma_start(wc_sb[:], W_common).then_inc(ld_small, 16)
            for col, b in ((0, b_left), (1, b_right)):
                sp.dma_start(blr[:, col:col + 1], b.rearrange("(a o) -> a o", a=1).broadcast_to([P, 1])).then_inc(ld_small, 16)

            def context_in(k):
                at = slice(CT * k, CT * (k + 1))
                sp.dma_start(ctx_sb[:, at], context_v[:, at]).then_inc(ld_ctx[k], 16)

            def x_in(k):
                at = slice(XT * k, XT * (k + 1))
                sp.dma_start(xt[:, at], x_v[:, at]).then_inc(ld_x[k], 16)

            for k in (0, 3, 4, 1):
                context_in(k)
            x_in(0)
            for k in (2, 5, 6, 7):
                context_in(k)
            load(0, 0)
            x_in(1)
            load(0, 1)
            x_in(2)
            load(0, 2)
            x_in(3)
            load(0, 3)
            sp.wait_ge(spares_set, 1)
            sp.dma_start(routed_rows[PADS:PADS + SPARE * TR].rearrange("(j p) w -> p j w", p=P), padt[:, 0:2 * SPARE]).then_inc(spares_out, 16)

            def loads(g, last):
                for c in range(C - RING if last else C):
                    sp.wait_ge(tested, g * C + (c + 1))
                    load(g + (1 if c >= C - RING else 0), (c + RING) % C)

            loads(0, False)
            with sp.Fori(1, 3) as g:
                loads(g, False)
            sp.wait_ge(ctxT_ps, PAIRS)
            sp.wait_ge(dots, 1)
            sp.dma_start(w1.rearrange("p (e h) -> p e h", e=E), W1.rearrange("e d h -> d e h")).then_inc(ld_w, 16)
            loads(3, False)
            sp.dma_start(w2.rearrange("p (e k d) -> p e k d", e=E, k=HB), W2.rearrange("e (k p) d -> p e k d", p=P)).then_inc(ld_w, 16)
            with sp.Fori(4, G - 1) as g:
                loads(g, False)
            loads(G - 1, True)

            def pads(e0, e1):
                sp.wait_ge(pads_known, 1)
                for e in range(e0, e1):
                    at = sp.value_load(pad_at[0:1, e:e + 1], min_val=e * REGION, max_val=e * REGION + N)
                    sp.dma_start(routed_rows[bass.ds(at, TR)].rearrange("(a p) w -> p a w", p=P), padt[:, 2 * e:2 * e + 2]).then_inc(pads_out, 16)

            def all_rows_out():
                sp.wait_ge(pads_out, 16 * E)
                sp.wait_ge(table_ok, 2)
                sp.wait_ge(scattered, 16 * 2 * T)

            sp.wait_ge(tested, G * C)
            sp.wait_ge(early_out, 1)
            sp.wait_ge(table_ok, 1)

            def rows_in(h, q):
                if not (isinstance(h, int) and UNROLL * h + q < XS):
                    sp.wait_ge(row_info, UNROLL * h + (q + 1 - XS))
                at = sp.value_load(table[0:1, 1, bass.ds(UNROLL * h + q, 1)], min_val=0, max_val=PADS + (SPARE - 1) * TR)
                sp.dma_start(xs[:, q % XS], routed_rows[bass.ds(at, TR)].rearrange("(a p) w -> p a w", p=P)).then_inc(xs_ld[q % XS], 16)

            steps(sp, rows_in, {12: (lambda: pads(0, 3),), 13: (lambda: pads(3, 6),), 14: (lambda: pads(6, E),),
                                EARLY: (all_rows_out,)})
            for q in range(UNROLL):
                sp.wait_ge(sent[q], 32 * ((NT - q + UNROLL - 1) // UNROLL))
            for k in range(4):
                for o in range(2):
                    sp.dma_start(res[:, o, 8 * k:8 * k + 8],
                                 results[o * N + k * 8 * P:o * N + (k + 1) * 8 * P].rearrange("(t p) d -> p t d", p=P)).then_inc(res_ld[k], 16)
            for k in range(4):
                sp.wait_ge(summed, k + 1)
                sp.dma_start(out_v[:, 8 * k:8 * k + 8], res[:, 0, 8 * k:8 * k + 8]).then_inc(stored, 16)
            sp.wait_ge(stored, 16 * 4)

        @block.gpsimd
        def _(pool):
            own = Count(pool, pool_own)
            for c, (s, n) in enumerate(((masked, DEEP), (p_free, DEEP), (turned, DEEP * JB), (sums_free, 2))):
                nc.gpsimd.memset(held[:, c + 1:c + 2], 0.0).then_inc(s, n)
            nc.gpsimd.memset(ones[:], 1.0).then_inc(pool_own, 1)
            own.n += 1
            own.mark(nc.gpsimd.memset(onesb[:], 1.0))
            for t, value in ((quarter_d, D / 4.0), (inverse_d, 1.0 / D), (eps, EPS)):
                own.mark(nc.gpsimd.memset(t[:], value))
            own(nc.gpsimd.memset(padt[:], 0.0))
            for dst, src, op in ((ident, ones, ALU.is_equal), (identb, onesb, ALU.is_equal)):
                nc.gpsimd.affine_select(out=dst[:], in_=src[:], compare_op=op, fill=0.0, base=0,
                                        pattern=[[-1, P]], channel_multiplier=1).then_inc(consts, 1)
            nc.gpsimd.memset(half[:], -0.5).then_inc(consts, 1)
            nc.gpsimd.affine_select(out=before[:], in_=onesb[:], compare_op=ALU.is_gt, fill=0.0, base=0,
                                    pattern=[[1, P]], channel_multiplier=-1).then_inc(consts, 1)
            nc.gpsimd.memset(xh[:, :, D:DA], 1.0).then_inc(consts, 1)
            for t, pattern, base, mult in ((iota8[:], [[1, E]], 0, 0), (region0[:], [[REGION, E]], 0, 0), (carry[:], [[REGION, E]], 0, 0),
                                           (kk[:], [[1, NT]], 0, 0)):
                nc.gpsimd.iota(t, pattern=pattern, base=base, channel_multiplier=mult,
                               allow_small_or_imprecise_dtypes=True).then_inc(consts, 1)
            nc.gpsimd.iota(dest[:], pattern=[[P, T], [N, 2]], base=0, channel_multiplier=1,
                           allow_small_or_imprecise_dtypes=True).then_inc(consts, 1)
            nc.gpsimd.iota(padt[:, :, D], pattern=[[P, 2 * E]], base=2 * N + TR * E, channel_multiplier=1,
                           allow_small_or_imprecise_dtypes=True).then_inc(spares_set, 1)

            def moments(v, m, n, ready, k):
                own.mark(nc.gpsimd.tensor_tensor(m[0], v[1], v[4], ALU.add))
                own(nc.gpsimd.tensor_tensor(m[1], v[1], v[4], ALU.subtract))
                own.mark(nc.gpsimd.tensor_tensor(m[2], v[2], v[5], ALU.add))
                own(nc.gpsimd.tensor_tensor(m[3], m[1], m[1], ALU.mult))
                own.mark(nc.gpsimd.tensor_tensor(m[5], m[0], half[:, 0:n], ALU.mult))
                own(nc.gpsimd.tensor_tensor(m[4], m[3], quarter_d[:, 0:n], ALU.mult))
                own(nc.gpsimd.tensor_tensor(m[3], m[4], m[2], ALU.add))
                own(nc.gpsimd.tensor_tensor(m[4], m[3], inverse_d[:, 0:n], ALU.mult))
                own(nc.gpsimd.tensor_tensor(m[3], m[4], eps[:, 0:n], ALU.add))
                nc.gpsimd.tensor_tensor(m[6], m[3], half[:, 0:n], ALU.pow).then_inc(ready, 1)
                pool.wait_ge(ready, k + 1)
                nc.gpsimd.tensor_tensor(m[7], m[5], m[6], ALU.mult).then_inc(ready, 1)

            def x_moments(k):
                pool.wait_ge(x_stats, k + 1)
                at = slice(XT * k, XT * (k + 1))
                moments([stats[:, at, n] for n in range(6)], [ms[:, n, at] for n in range(8)], XT, x_norm_ok, 2 * k - 2)

            pool.wait_ge(consts, 3)
            pool.wait_ge(var_ready, 1)
            nc.gpsimd.tensor_tensor(ms[:, 5, 0:XT], ms[:, 4, 0:XT], half[:, 0:XT], ALU.pow).then_inc(rstd_ready, 1)
            pool.wait_ge(rowmax, 1)
            nc.gpsimd.partition_all_reduce(rmax[:, 1:2], rmax[:, 0:1], P, bass.bass_isa.ReduceOp.max).then_inc(allmax, 1)

            def diagonal(g):
                nc.gpsimd.tensor_tensor(diag[:], ident[:].unsqueeze(1).broadcast_to([P, IT, P]),
                                        beta[:, bass.ds(IT * g, IT)].unsqueeze(2).broadcast_to([P, IT, P]), ALU.mult).then_inc(diag_ready, 1)

            pool.wait_ge(beta_ok, 1)
            diagonal(0)
            x_moments(1)

            def carry_wait(done):
                pool.wait_ge(pool_held, done + 1)
                nc.gpsimd.tensor_tensor(held[:, 0:1], held[:, 0:1], held[:, 0:1], ALU.mult).then_inc(pool_held, 1)

            nc.gpsimd.memset(held[:, 0:1], 0.0).then_inc(pool_held, 1)

            def next_diagonal(g):
                pool.wait_ge(brow_ps, g + 1)
                diagonal(g + 1)

            def post_moments(g, k):
                pool.wait_ge(stats_ok, 2 * g + (k + 1))
                moments([post_stats[:, k, :, n] for n in range(6)], [pm[:, k, n] for n in range(8)], IT, norm_ok, 4 * g + 2 * k)

            def scatter(g, i):
                for k in range(2):
                    pool.indirect_dma_start(out=routed_rows, out_offset=bass.IndirectOffsetOnAxis(ap=slot[:, i, k:k + 1], axis=0),
                                            in_=pay[:, i, k], in_offset=None).then_inc(scattered, 16)

            def add_to_x(g):
                pool.wait_ge(relu_ok, g + 1)
                nc.gpsimd.tensor_tensor(xt[:, bass.ds(IT * g, IT)], xt[:, bass.ds(IT * g, IT)], y1[:], ALU.add).then_inc(x_new, 1)

            def destinations(g, done=None):
                own(nc.gpsimd.tensor_copy(pay[:, :, :, D], dest[:, bass.ds(IT * g, IT)]))
                pool.wait_ge(xn_ready, g + 1)
                pool.wait_ge(slot_ok, g + 1)
                carry_wait(g if done is None else done)

            def post(g, rows_before=True, diagonal_too=True):
                add_to_x(g)
                post_moments(g, 0)
                if diagonal_too:
                    next_diagonal(g + 1)
                if rows_before:
                    pool.wait_ge(scattered, 16 * 2 * IT * g)
                post_moments(g, 1)
                destinations(g)
                for i in range(IT):
                    scatter(g, i)

            def low_w1(e):
                at = slice(e * H, (e + 1) * H)
                pool.wait_ge(w1_high, e + 1)
                nc.gpsimd.tensor_tensor(w1[:, at], w1[:, at], w1_hi[:, at], ALU.subtract).then_inc(w1_split, 1)

            def last_power(k):
                pool.wait_ge(last_var, k + 1)
                nc.gpsimd.tensor_tensor(pm[:, k, 6], pm[:, k, 3], half[:, 0:IT], ALU.pow).then_inc(norm_ok, 2)

            next_diagonal(0)
            x_moments(2)
            x_moments(3)
            pool.dma_start(wr_sb[:], Wr).then_inc(ld_bias, 16)
            with nc.allow_non_contiguous_dma(reason="1024 elements each"):
                pool.dma_start(gcol[:], ln_g.rearrange("e d -> d e")).then_inc(ld_bias, 16)
                pool.dma_start(bcol[:], ln_b.rearrange("e d -> d e")).then_inc(ld_bias, 16)
            pool.dma_start(br_row[:], br.rearrange("(a e) -> a e", a=1).broadcast_to([P, E])).then_inc(ld_bias, 16)
            pool.dma_start(b2_row[:], b2.rearrange("(a e) d -> a (e d)", a=1).broadcast_to([P, E * D])).then_inc(ld_bias, 16)
            with nc.allow_non_contiguous_dma(reason="4096 elements"):
                pool.dma_start(b1c[:].rearrange("p (e j) -> p e j", e=E), b1.rearrange("e (j p) -> p e j", p=P)).then_inc(ld_bias, 16)
            pool.wait_ge(spares_out, 16)
            nc.gpsimd.iota(padt[:, :, D], pattern=[[P, 2 * E]], base=2 * N, channel_multiplier=1,
                           allow_small_or_imprecise_dtypes=True).then_inc(consts, 1)
            post(0, rows_before=False)
            with pool.Fori(1, G - 2) as g:
                own.enter(g - 1, POOL_OWN)
                post(g)
                own.leave(G - 3)
            add_to_x(G - 2)
            post_moments(G - 2, 0)
            for e in range(3):
                low_w1(e)
            pool.wait_ge(scattered, 16 * 2 * IT * (G - 2))
            nc.gpsimd.memset(held[:, 5:6], 0.0).then_inc(early_out, 1)
            post_moments(G - 2, 1)
            for e in range(3, E):
                low_w1(e)
            destinations(G - 2)
            scatter(G - 2, 0)
            scatter(G - 2, 1)
            last_power(0)
            scatter(G - 2, 2)
            scatter(G - 2, 3)

            ROWS_AT = 5

            def second_power():
                pool.wait_ge(scattered, 16 * 2 * IT * (G - 1))
                last_power(1)

            def last_rows():
                destinations(G - 1, G - 1 + ROWS_AT)
                scatter(G - 1, 0)
                scatter(G - 1, 1)

            def last_rows_too():
                scatter(G - 1, 2)
                scatter(G - 1, 3)

            def send(h, q):
                pool.wait_ge(y_gated, UNROLL * h + (q + 1))
                carry_wait(UNROLL * h + (q + G - (1 if isinstance(h, int) and UNROLL * h + q < ROWS_AT else 0)))
                for a in range(2):
                    pool.indirect_dma_start(out=results, out_offset=bass.IndirectOffsetOnAxis(ap=dq[:, q, a:a + 1], axis=0),
                                            in_=yo[:, q, a], in_offset=None).then_inc(sent[q], 16)

            steps(pool, send, {2: (second_power,), ROWS_AT: (last_rows,), ROWS_AT + 1: (last_rows_too,)})

        @block.scalar
        def _(act):
            own = Count(act, act_own)
            act.wait_ge(folded, 2)
            nc.scalar.activation(wrows[:].rearrange("p o k -> p (o k)"), ps[:, 4], ACT.Copy).then_inc(rows_sb, 1)
            for n in range(PAIRS):
                act.wait_ge(ctxT_ps, n + 1)
                if n >= 2:
                    act.wait_ge(ctxT_used, n - 1)
                nc.scalar.activation(ctxT[:, n % 2], ps[:, 5 + n % 2], ACT.Copy).then_inc(ctxT_sb, 1)
            act.wait_ge(allmax, 2)
            nc.scalar.activation(uv[:, 0], lr[:, 1], ACT.Exp, bias=rmax[:, 2:3]).then_inc(u_ready, 1)
            nc.scalar.activation(uv[:, 1], lr[:, 1], ACT.Exp, bias=rmax[:, 3:4], scale=SLOPE).then_inc(u_ready, 1)
            act.wait_ge(beta_in, 1)
            nc.scalar.activation(beta[:], lR[:], ACT.Exp, scale=SLOPE - 1.0).then_inc(beta_ok, 1)
            act.wait_ge(u_ready, 3)

            def save_sums(g):
                for k, (s, n) in enumerate(((first_sums, g + 1), (p_free, g * NB + (NB + DEEP)))):
                    act.wait_ge(s, n)
                    nc.scalar.activation(gsum[:, 2 * k:2 * k + 2].rearrange("p b d -> p (b d)"),
                                         ps[:, SUMS + k, 0:2 * DA], ACT.Copy).then_inc(sums_free, 1)

            def post_relu(g):
                act.wait_ge(rden_ok, g + 1)
                for i in range(IT):
                    last = nc.scalar.activation(y1[:, i], gsum[:, i, 0:D], ACT.Relu, scale=rden[:, i:i + 1])
                last.then_inc(relu_ok, 1)

            def post_norm(g, last=False):
                if last:
                    act.wait_ge(last_bias, 1)
                else:
                    act.wait_ge(norm_ok, 4 * g + 2)
                for i in range(IT):
                    last = nc.scalar.activation(y1[:, i], xt[:, bass.ds(IT * g + i, 1)].rearrange("p a d -> p (a d)"), ACT.Identity,
                                                scale=pm[:, 0, 6, i:i + 1], bias=pm[:, 0, 7, i:i + 1])
                last.then_inc(y_ready, 1)

            def post_T(g):
                act.wait_ge(yT_ps, g + 1)
                nc.scalar.activation(yT[:], ps[:, Y_T], ACT.Copy).then_inc(yT_sb, 1)

            def post_tokens(g, last=False):
                if last:
                    act.wait_ge(last_bias, 2)
                else:
                    act.wait_ge(norm_ok, 4 * g + 4)
                for i in range(IT):
                    last = nc.scalar.activation(pay[:, i, 0, 0:D], y1[:, i], ACT.Identity,
                                                scale=pm[:, 1, 6, i:i + 1], bias=pm[:, 1, 7, i:i + 1])
                own(last)
                nc.scalar.activation(pay[:, :, 1, 0:D], pay[:, :, 0, 0:D], ACT.Copy).then_inc(xn_ready, 1)

            def post_exp(g):
                act.wait_ge(lg_in, g + 1)
                nc.scalar.activation(lg[:], lgs[:], ACT.Exp).then_inc(lg_exp, 1)

            services = {2: save_sums, 7: post_relu, 17: post_norm, 21: post_T, 25: post_tokens, 27: post_exp}

            LN_NORMAL = {b + n: 8 * k + 2 * n for k, b in ((1, 6), (2, 13), (3, 21)) for n in range(4)}

            def normal_x(t):
                if t % XT == 0:
                    act.wait_ge(x_norm_ok, 2 * (t // XT))
                for t in (t, t + 1):
                    nc.scalar.activation(xh[:, t, 0:D], xt[:, t], ACT.Identity, scale=ms[:, 6, t:t + 1], bias=ms[:, 7, t:t + 1]).then_inc(xh_ok, 1)

            def scale_w1(e):
                act.wait_ge(lnb_ps, e + 1)
                at = slice(e * H, (e + 1) * H)
                nc.scalar.activation(w1[:, at], w1[:, at], ACT.Copy, scale=gcol[:, e:e + 1]).then_inc(w1_scaled, 1)

            def high_w1(e):
                act.wait_ge(w1_scaled, e + 1)
                at = slice(e * H, (e + 1) * H)
                nc.scalar.activation(w1_hi[:, at].bitcast(FP32R), w1[:, at], ACT.Copy).then_inc(w1_high, 1)

            def group(g, before_it, last=False):
                act.wait_ge(brow_ps, g + 1)
                if before_it:
                    act.wait_ge(t_ready, g * NB)
                own(nc.scalar.activation(beta_row[:], ps[:, BETA], ACT.Copy))
                for b in range(NB):
                    if before_it and b in services:
                        services[b](g - 1)
                    if not before_it and b in LN_NORMAL:
                        normal_x(LN_NORMAL[b])
                    if last and 6 <= b < 6 + 3 * E and b % 3 < 2:
                        (high_w1 if b % 3 else scale_w1)((b - 6) // 3)
                    act.wait_ge(masked, g * NB + (b + 1))
                    nc.scalar.activation(tbuf[:, b % DEEP], beta_row[:], ACT.Relu, bias=uv[:, 2, b:b + 1],
                                         scale=uv[:, 1, b:b + 1]).then_inc(t_ready, 1)

            group(0, False)
            with act.Fori(1, G - 1) as g:
                own.enter(g - 1, ACT_OWN)
                group(g, True)
                own.leave(G - 2)
            group(G - 1, True, last=True)
            save_sums(G - 1)

            def turn_out(h, q):
                if not (isinstance(h, int) and UNROLL * h + q < 2):
                    act.wait_ge(h_ps, UNROLL * h + (q - 1))
                act.wait_ge(x_turned, UNROLL * h + (q + 1))
                nc.scalar.activation(xT_hi[:, q % 2], ps[:, psX, 0:TR], ACT.Copy).then_inc(xT_sb, 1)

            def gelu(h, q):
                e = act.value_load(table[0:1, 0, bass.ds(UNROLL * h + q, 1)], min_val=0, max_val=E - 1)
                if not (isinstance(h, int) and UNROLL * h + q < 2):
                    act.wait_ge(y_ps, UNROLL * h + (q - 1))
                act.wait_ge(h_ps, UNROLL * h + (q + 1))
                for j in range(HB):
                    last = nc.scalar.activation(hT[:, q % 2, j], ps[:, psH + 2 * (q % 2) + j // 2, (j % 2) * TR:(j % 2 + 1) * TR],
                                                ACT.Gelu, bias=b1c[:, bass.ds(e * HB + j, 1)])
                last.then_inc(h_gelu, 1)

            def gate(h, q):
                act.wait_ge(y_added, UNROLL * h + (q + 1))
                for a in range(2):
                    last = nc.scalar.activation(yo[:, q, a], yb[:, q % 2, a], ACT.Copy, scale=gq[:, q, a:a + 1])
                last.then_inc(y_gated, 1)

            act.wait_ge(bias_ready, 1)
            act.wait_ge(table_ok, 1)
            turn_out(0, 0)
            post_relu(G - 1)
            turn_out(0, 1)

            def step(h, q):
                gelu(h, q)
                if exists(h, q + 2):
                    turn_out(*shifted(h, q, 2))
                if exists(h, q - 1):
                    gate(*shifted(h, q, -1))

            between = {2: (lambda: post_norm(G - 1, last=True),),
                       3: (lambda: post_T(G - 1),),
                      5: (lambda: post_exp(G - 1),),
                      6: (lambda: post_tokens(G - 1, last=True),),
                      EARLY: (lambda: act.wait_ge(table_ok, 2),)}
            steps(act, step, between)
            gate((NT - 1) // UNROLL, (NT - 1) % UNROLL)

        @block.vector
        def _(dve):
            own = Count(dve, dve_own)

            def centre(a, n):
                v = [stats[:, a:a + n, k] for k in range(6)]
                m = [ms[:, k, a:a + n] for k in range(6)]
                own.mark(nc.vector.tensor_tensor(m[0], v[1], v[4], ALU.add))
                own.mark(nc.vector.tensor_tensor(m[1], v[1], v[4], ALU.subtract))
                own(nc.vector.tensor_tensor(m[2], v[2], v[5], ALU.add))
                own.mark(nc.vector.tensor_scalar(m[3], m[0], 0.5, None, ALU.mult))
                own(nc.vector.tensor_tensor(m[5], m[1], m[1], ALU.mult))
                own(nc.vector.scalar_tensor_tensor(m[0], m[5], D / 4.0, m[2], ALU.mult, ALU.add))
                nc.vector.tensor_scalar(m[4], m[0], 1.0 / D, EPS, ALU.mult, ALU.add).then_inc(var_ready, 1)

            dve.wait_ge(folded, 1)
            nc.vector.tensor_copy(wck[:].rearrange("p k o -> p (k o)"), ps[:, 1, 0:2 * KC]).then_inc(folded_sb, 1)
            def stats_of(t):
                dve.wait_ge(ld_x[t // XT], 16)
                for t in range(t, t + XT // 2):
                    own.mark(nc.vector.bn_stats(stats[:, t], xt[:, t]))
                if (t + 1) % XT == 0:
                    own.wait()
                    nc.vector.memset(hold[:], 0.0).then_inc(x_stats, 1)

            def first_normal():
                dve.wait_ge(rstd_ready, 1)
                for t in range(XT):
                    own.mark(nc.vector.tensor_scalar(xh[:, t, 0:D], xt[:, t], ms[:, 3, t:t + 1], ms[:, 5, t:t + 1],
                                                     ALU.subtract, ALU.mult))
                own.wait()

            def test(g, c, k):
                if k == 0:
                    dve.wait_ge(adj_ld[c % RING], 16 * (g * (C // RING) + (c // RING + 1)))
                    dve.wait_ge(turned, g * NB + (c + 1) * JB)
                at = slice(k * IT // 2, (k + 1) * IT // 2)
                ins = nc.vector.tensor_scalar(mring[:, c % RING, at], ring[:, c % RING, at], 0.0, None, ALU.is_gt)
                if k == 1:
                    ins.then_inc(tested, 1)

            dve.wait_ge(rows_sb, 1)
            for t in range(2 * PAIRS, T):
                if t == 20:
                    stats_of(0)
                    stats_of(XT // 2)
                    centre(0, XT)
                if t % CT == 0 or t == 2 * PAIRS:
                    dve.wait_ge(ld_ctx[t // CT], 16)
                for o in range(2):
                    own.mark(nc.vector.scalar_tensor_tensor(junk[:, o], ctx_sb[:, t], 1.0, wrows[:, o], ALU.mult, ALU.mult,
                                                            accum_out=lr[:, o, t:t + 1]))
                    if (t, o) != (2 * PAIRS, 0):
                        own.wait(1)
            own.wait()
            nc.vector.memset(hold[:], 0.0).then_inc(dots, 1)
            test(0, 0, 0)
            test(0, 0, 1)
            dve.wait_ge(ctxT_used, PAIRS)
            dve.wait_ge(ld_small, 5 * 16)
            for o in (1, 0):
                own.mark(nc.vector.tensor_scalar(lr[:, o, 2 * PAIRS:T], lr[:, o, 2 * PAIRS:T], blr[:, o:o + 1], None, ALU.add))
                own.mark(nc.vector.tensor_scalar(lr[:, o, 0:2 * PAIRS],
                                                 ps[:, 0, 0:4 * PAIRS].rearrange("p (t o) -> p o t", o=2)[:, o],
                                                 blr[:, o:o + 1], None, ALU.add))
            own.wait()
            nc.vector.tensor_reduce(rmax[:, 0:1], lr[:, 1], AX_X, ALU.max).then_inc(rowmax, 1)
            dve.wait_ge(allmax, 1)
            own.mark(nc.vector.tensor_scalar(rmax[:, 2:3], rmax[:, 1:2], -1.0, None, ALU.mult))
            nc.vector.tensor_scalar(rmax[:, 3:4], rmax[:, 1:2], -SLOPE, None, ALU.mult).then_inc(allmax, 1)
            nc.vector.tensor_scalar(lR[:], lr[:, 0], rmax[:, 1:2], 0.0, ALU.add, ALU.max).then_inc(beta_in, 1)
            dve.wait_ge(u_ready, 1)
            nc.vector.tensor_scalar(uv[:, 2], uv[:, 0], -1.0, None, ALU.mult).then_inc(u_ready, 1)

            first_normal()
            test(0, 1, 0)
            test(0, 1, 1)

            def post_sums(g):
                dve.wait_ge(sums_free, 2 * g + 4)
                nc.vector.reciprocal(rden[:], gsum[:, :, D]).then_inc(rden_ok, 1)

            def post_stats_of(g, k, i):
                if i == 0:
                    dve.wait_ge(y_ready if k else x_new, g + 1)
                    nc.vector.memset(hold[:], 0.0)
                for n in (i, i + 1):
                    ins = nc.vector.bn_stats(post_stats[:, k, n], y1[:, n] if k else xt[:, IT * g + n])
                    own.mark(ins)
                if i == 2:
                    own.wait()
                    nc.vector.memset(hold[:], 0.0).then_inc(stats_ok, 1)

            def post_logits(g):
                dve.wait_ge(lg_ps, g + 1)
                own.mark(nc.vector.tensor_tensor(lg[:], ps[:, Y_T, 0:IT * E].rearrange("p (i e) -> p i e", i=IT),
                                                 br_row[:].unsqueeze(1).broadcast_to([P, IT, E]), ALU.add))

            def post_logits_max(g):
                own.wait()
                own(nc.vector.tensor_reduce(rtop[:], lg[:], AX_X, ALU.max))
                nc.vector.tensor_tensor(lgs[:], lg[:], rtop[:].unsqueeze(2).broadcast_to([P, IT, E]), ALU.subtract).then_inc(lg_in, 1)

            def post_top(g):
                dve.wait_ge(lg_exp, g + 1)
                nc.vector.memset(hold[:], 0.0)
                for i in range(IT):
                    own.mark(nc.vector.max(top[:, i], lg[:, i]))

            def post_which(g):
                own.wait()
                nc.vector.memset(hold[:], 0.0)
                for i in range(IT):
                    own.mark(nc.vector.max_index(topi[:, i], top[:, i], lg[:, i]))
                own.mark(nc.vector.tensor_tensor(rtop[:], top[:, :, 0], top[:, :, 1], ALU.add))

            def post_chosen(g):
                dve.wait_ge(norm_ok, 4 * g + 3)
                own.wait()
                own.mark(nc.vector.reciprocal(rtop[:], rtop[:]))
                own(nc.vector.tensor_tensor(chosen[:], iota8[:].unsqueeze(1).unsqueeze(1).broadcast_to([P, IT, 2, E]),
                                            topi[:, :, 0:2].unsqueeze(3).broadcast_to([P, IT, 2, E]), ALU.is_equal))
                nc.vector.tensor_tensor(either[:], chosen[:, :, 0], chosen[:, :, 1], ALU.add).then_inc(either_ok, 1)
                own.mark(nc.vector.tensor_tensor(pay[:, :, :, D + 1], top[:, :, 0:2],
                                                 rtop[:].unsqueeze(2).broadcast_to([P, IT, 2]), ALU.mult))

            def post_slots(g):
                dve.wait_ge(rank_ps, g + 1)
                own(nc.vector.tensor_tensor(place[:], ps[:, Y_T, 64:64 + IT * E].rearrange("p (i e) -> p i e", i=IT),
                                            carry[:].unsqueeze(1).broadcast_to([P, IT, E]), ALU.add))
                own.mark(nc.vector.tensor_tensor(carry[:], carry[:], ps[:, Y_T, 64 + IT * E:64 + IT * E + E], ALU.add))
                own.mark(nc.vector.tensor_tensor(picked[:], chosen[:], place[:].unsqueeze(2).broadcast_to([P, IT, 2, E]), ALU.mult))

            def post_slots_out(g):
                own.wait()
                own(nc.vector.tensor_reduce(slotf[:], picked[:], AX_X, ALU.add))
                nc.vector.tensor_copy(slot[:], slotf[:]).then_inc(slot_ok, 1)

            def fold_b1():
                dve.wait_ge(lnb_ps, E)
                nc.vector.tensor_tensor(b1c[:], b1c[:], ps[:, BETA, 0:E * HB], ALU.add).then_inc(bias_ready, 1)

            def post_x(g):
                dve.wait_ge(relu_ok, g + 1)
                rows = slice(IT * g, IT * (g + 1))
                nc.vector.tensor_tensor(xt[:, rows], xt[:, rows], y1[:], ALU.add).then_inc(x_new, 1)

            def post_moments(g, k):
                post_stats_of(g, k, 0)
                post_stats_of(g, k, 2)
                v = [post_stats[:, k, :, n] for n in range(6)]
                m = [pm[:, k, n] for n in range(8)]
                own.mark(nc.vector.tensor_tensor(m[0], v[1], v[4], ALU.add))
                own.mark(nc.vector.tensor_tensor(m[1], v[1], v[4], ALU.subtract))
                own(nc.vector.tensor_tensor(m[2], v[2], v[5], ALU.add))
                own.mark(nc.vector.tensor_scalar(m[5], m[0], -0.5, None, ALU.mult))
                own(nc.vector.tensor_tensor(m[3], m[1], m[1], ALU.mult))
                own(nc.vector.scalar_tensor_tensor(m[4], m[3], D / 4.0, m[2], ALU.mult, ALU.add))
                nc.vector.tensor_scalar(m[3], m[4], 1.0 / D, EPS, ALU.mult, ALU.add).then_inc(last_var, 1)

            def post_bias(g, k):
                m = [pm[:, k, n] for n in range(8)]
                dve.wait_ge(norm_ok, 4 * g + (2 * k + 2))
                nc.vector.tensor_tensor(m[7], m[5], m[6], ALU.mult).then_inc(last_bias, 1)

            def count_tiles(over):
                own(nc.vector.tensor_tensor(ntile[:, 0], carry[:], region0[:], ALU.subtract))
                own(nc.vector.tensor_scalar(ntile_i[:, 0], ntile[:, 0], float(over), None, ALU.add))
                own(nc.vector.tensor_scalar(ntile_i[:, 1], ntile_i[:, 0], TR.bit_length() - 1, None, ALU.logical_shift_right))
                own(nc.vector.tensor_copy(ntile[:, 1], ntile_i[:, 1]))

            def first_sums_of_tiles():
                own.mark(nc.vector.tensor_scalar(ntile[:, 2], ntile[:, 1], -float(TR), float(REGION), ALU.mult, ALU.add))
                own(nc.vector.tensor_copy(ntile[:, 3, 0:1], ntile[:, 1, 0:1]))
                sum_tiles(1, E // 2)

            def sum_tiles(e0, e1):
                for e in range(e0, e1):
                    own(nc.vector.tensor_tensor(ntile[:, 3, e:e + 1], ntile[:, 3, e - 1:e], ntile[:, 1, e:e + 1], ALU.add))

            def compare_tiles(n):
                shape = [P, E, n]
                own(nc.vector.tensor_tensor(cmp[:, 0, :, 0:n], kk[:, 0:n].unsqueeze(1).broadcast_to(shape),
                                            ntile[:, 3].unsqueeze(2).broadcast_to(shape), ALU.is_ge))
                own(nc.vector.tensor_tensor(cmp[:, 1, :, 0:n], cmp[:, 0, :, 0:n], ntile[:, 2].unsqueeze(2).broadcast_to(shape), ALU.mult))
                for k in range(2):
                    own.mark(nc.vector.tensor_reduce(tab[:, k, 0:n], cmp[:, k, :, 0:n].rearrange("p e n -> p n e"), AX_X, ALU.add))

            def fill_table(k0, n):
                own.wait()
                own.mark(nc.vector.scalar_tensor_tensor(tab[:, 2, 0:n], kk[:, 0:n], float(TR), tab[:, 1, 0:n], ALU.mult, ALU.add))
                own(nc.vector.tensor_scalar(table[:, 0, k0:k0 + n], tab[:, 0, 0:n], float(E - 1), None, ALU.min))

            def take_early():
                own(nc.vector.tensor_tensor(taken[:, 1, 0:E], ntile[:, 3], ntile[:, 1], ALU.subtract))
                own(nc.vector.tensor_scalar(taken[:, 2, 0:E], taken[:, 1, 0:E], -1.0, float(EARLY), ALU.mult, ALU.add))
                own.mark(nc.vector.memset(taken[:, 0, E:E + 1], 0.0))
                own(nc.vector.scalar_tensor_tensor(taken[:, 0, 0:E], taken[:, 2, 0:E], 0.0, ntile[:, 1], ALU.max, ALU.min))

            def fill_early():
                fill_table(0, EARLY)
                nc.vector.tensor_copy(table[:, 1, 0:EARLY], tab[:, 2, 0:EARLY]).then_inc(table_ok, 1)

            early_table = {4: lambda: count_tiles(0), 10: first_sums_of_tiles, 11: lambda: sum_tiles(E // 2, E), 13: take_early,
                           14: lambda: compare_tiles(EARLY), 15: fill_early, 20: fold_b1}

            services = {3: post_sums,
                        8: lambda g: post_stats_of(g, 0, 0), 9: lambda g: post_stats_of(g, 0, 2),
                        16: lambda g: post_stats_of(g, 1, 0), 17: lambda g: post_stats_of(g, 1, 2),
                        22: post_logits, 23: post_logits_max, 25: post_top, 26: post_which, 27: post_chosen,
                        30: post_slots, 31: post_slots_out}

            LN_STATS = {0: 8, 1: 12, 6: 16, 7: 20, 14: 24, 15: 28}

            def group(g, first, last):
                for b in range(NB):
                    c = b // JB + 2
                    if b % JB >= 2 and not (last and c >= C):
                        test(g + c // C, c % C, b % JB - 2)
                    if first:
                        if b in LN_STATS:
                            stats_of(LN_STATS[b])
                    elif b in services:
                        services[b](g - 1)
                    if last and b in early_table:
                        early_table[b]()
                    dve.wait_ge(turned, g * NB + (b + 1 + DEEP * JB))
                    dve.wait_ge(t_ready, g * NB + (b + 1))
                    dve.wait_ge(p_free, g * NB + (b + 1))
                    nc.vector.scalar_tensor_tensor(pbuf[:, b % DEEP], tbuf[:, b % DEEP], uv[:, 0, b:b + 1],
                                                   ps[:, TURN + b % DEEP].bitcast(BF16)[:, 0:GI],
                                                   ALU.add, ALU.mult).then_inc(masked, 1)

            group(0, True, False)
            dve.wait_ge(ld_bias, 6 * 16)
            dve.wait_ge(consts, 10)
            with dve.Fori(1, G - 1) as g:
                own.enter(g - 1, POST_OWN)
                group(g, False, False)
                own.leave(G - 2)
            group(G - 1, False, True)
            post_sums(G - 1)

            def count_last():
                own.wait()
                nc.vector.tensor_copy(pad_at[:], carry[:]).then_inc(pads_known, 1)
                count_tiles(TR - 1)
                own(nc.vector.tensor_tensor(ntile[:, 1], ntile[:, 1], taken[:, 0, 0:E], ALU.subtract))
                own(nc.vector.tensor_tensor(taken[:, 1, 0:E], taken[:, 0, 1:E + 1], taken[:, 0, 0:E], ALU.subtract))

            def sum_last():
                sum_tiles(E // 2, E)
                own(nc.vector.scalar_tensor_tensor(ntile[:, 2], taken[:, 1, 0:E], float(TR), ntile[:, 2], ALU.mult, ALU.add))

            def fill_last():
                fill_table(EARLY, NT - EARLY)
                nc.vector.scalar_tensor_tensor(table[:, 1, EARLY:NT], taken[:, 0, 0:1].broadcast_to([P, NT - EARLY]), float(TR),
                                               tab[:, 2, 0:NT - EARLY], ALU.mult, ALU.add).then_inc(table_ok, 1)
                dve.wait_ge(table_ok, 2)

            def fetch_w1(h, q):
                e = dve.value_load(table[0:1, 0, bass.ds(UNROLL * h + q, 1)], min_val=0, max_val=E - 1)
                if not (isinstance(h, int) and UNROLL * h + q < 2):
                    dve.wait_ge(h_ps, UNROLL * h + (q - 1))
                nc.vector.tensor_copy(w1e[:, q % 2, 0], w1_hi[:, bass.ds(e * H, H)])
                nc.vector.tensor_copy(w1e[:, q % 2, 1], w1[:, bass.ds(e * H, H)]).then_inc(w1_there, 1)

            def low_part(h, q):
                dve.wait_ge(xT_sb, UNROLL * h + (q + 1))
                nc.vector.tensor_tensor(xT_lo[:, q % 2], ps[:, psX, 0:TR], xT_hi[:, q % 2].bitcast(FP32), ALU.subtract).then_inc(x_low, 1)

            def info(h, q):
                if not (isinstance(h, int) and h == 0):
                    dve.wait_ge(sent[q], 32 * h)
                dve.wait_ge(xs_ld[q % XS], 16 * (UNROLL // XS) * h + 16 * (q // XS + 1))
                nc.vector.tensor_copy(dq[:, q], xs[:, q % XS, :, D])
                nc.vector.tensor_copy(gq[:, q], xs[:, q % XS, :, D + 1]).then_inc(row_info, 1)

            def out_y(h, q):
                e = dve.value_load(table[0:1, 0, bass.ds(UNROLL * h + q, 1)], min_val=0, max_val=E - 1)
                dve.wait_ge(y_ps, UNROLL * h + (q + 1))
                if not (isinstance(h, int) and UNROLL * h + q < 2):
                    dve.wait_ge(y_gated, UNROLL * h + (q - 1))
                nc.vector.tensor_tensor(yb[:, q % 2], ps[:, psY[q % 2], 0:2 * D].rearrange("p (a d) -> p a d", a=2),
                                        b2_row[:, bass.ds(e * D, D)].unsqueeze(1).broadcast_to([P, 2, D]), ALU.add).then_inc(y_added, 1)

            dve.wait_ge(tested, G * C)
            dve.wait_ge(table_ok, 1)
            dve.wait_ge(w1_split, E)
            fetch_w1(0, 0)
            low_part(0, 0)
            post_x(G - 1)
            fetch_w1(0, 1)
            low_part(0, 1)
            post_moments(G - 1, 0)

            def step(h, q):
                info(h, q)
                if exists(h, q - 1):
                    out_y(*shifted(h, q, -1))
                if exists(h, q + 2):
                    fetch_w1(*shifted(h, q, 2))
                    low_part(*shifted(h, q, 2))

            def serve(*at):
                return [lambda b=b: services[b](G - 1) for b in at]

            between = {2: (lambda: post_bias(G - 1, 0),), 3: (lambda: post_moments(G - 1, 1),),
                      4: serve(22, 23), 5: (lambda: post_bias(G - 1, 1), *serve(25, 26, 27)), 6: serve(30, 31),
                      7: (count_last,), 8: (first_sums_of_tiles,), 9: (sum_last,),
                       10: (lambda: compare_tiles(NT - EARLY),), 11: (fill_last,)}
            steps(dve, step, between)
            out_y(LAST, NT - UNROLL * LAST - 1)

            for k in range(4):
                at = slice(8 * k, 8 * k + 8)
                dve.wait_ge(res_ld[k], 32)
                own(nc.vector.tensor_tensor(res[:, 0, at], res[:, 0, at], res[:, 1, at], ALU.add))
                nc.vector.tensor_tensor(res[:, 0, at], res[:, 0, at], xt[:, at], ALU.add).then_inc(summed, 1)

        @block.tensor
        def _(pe):
            pe.wait_ge(ld_small, 5 * 16)
            for k in range(KC):
                last = nc.tensor.matmul(ps[:, 1, 2 * k:2 * k + 2], wc_sb[:, k * P:(k + 1) * P], wlr[:], start=True, stop=True)
            last.then_inc(folded, 1)
            for o in range(2):
                last = nc.tensor.matmul(ps[:, 4, o * KC * P:(o + 1) * KC * P], wlr[:, o:o + 1].broadcast_to([P, P]), wc_sb[:],
                                        start=True, stop=True)
            last.then_inc(folded, 1)
            pe.wait_ge(folded_sb, 1)
            pe.wait_ge(consts, 2)

            def context_dot(n):
                pe.wait_ge(ctxT_sb, n + 1)
                for i in range(2):
                    for k in range(KC):
                        last = nc.tensor.matmul(ps[:, 0, 2 * (2 * n + i):2 * (2 * n + i) + 2],
                                                ctxT[:, n % 2, (2 * i + k) * P:(2 * i + k + 1) * P], wck[:, k],
                                                start=(k == 0), stop=(k == KC - 1))
                last.then_inc(ctxT_used, 1)

            for n in range(PAIRS):
                if n % 2 == 0:
                    pe.wait_ge(ld_ctx[2 * n // CT], 16)
                if n >= 2:
                    pe.wait_ge(ctxT_sb, n - 1)
                for i in range(2):
                    for k in range(KC):
                        last = nc.tensor.transpose(ps[:, 5 + n % 2, (2 * i + k) * P:(2 * i + k + 1) * P],
                                                   ctx_sb[:, 2 * n + i, k * P:(k + 1) * P], ident[:])
                last.then_inc(ctxT_ps, 1)
                if n:
                    context_dot(n - 1)
            context_dot(PAIRS - 1)

            def beta_rows(g):
                pe.wait_ge(diag_ready, g + 1)
                nc.tensor.matmul(ps[:, BETA], ones[:], diag[:].rearrange("p a b -> p (a b)"), start=True, stop=True).then_inc(brow_ps, 1)

            def turn(g, b):
                c = b // JB
                if b % JB == 0:
                    pe.wait_ge(tested, g * C + (c + 1))
                pe.wait_ge(masked, g * NB + (b + 1))
                for i in range(IT):
                    last = nc.tensor.transpose(ps[:, TURN + b % DEEP].bitcast(BF16)[:, i * P:(i + 1) * P],
                                               mring[:, c % RING, i, (b % JB) * P:(b % JB + 1) * P], identb[:])
                last.then_inc(turned, 1)

            def add_up(g, b, first):
                pe.wait_ge(masked, g * NB + (b + 1 + DEEP))
                if first and b >= XT:
                    pe.wait_ge(xh_ok, b - XT + 1)
                for i in range(IT):
                    if b == 0 and i % 2 == 0:
                        pe.wait_ge(sums_free, 2 * g + (i // 2 + 1))
                    at = ps[:, SUMS + i // 2, (i % 2) * DA:(i % 2 + 1) * DA]
                    last = nc.tensor.matmul(at, pbuf[:, b % DEEP, i * P:(i + 1) * P], xh[:, b],
                                            start=(b == 0 and i % 2 == 0), stop=(b == NB - 1), skip_group_check=True)
                    if b == NB - 1 and i == 1:
                        last.then_inc(first_sums, 1)
                last.then_inc(p_free, 1)

            def post_T(g):
                pe.wait_ge(y_ready, g + 1)
                for i in range(IT):
                    last = nc.tensor.transpose(ps[:, Y_T, i * P:(i + 1) * P], y1[:, i], ident[:])
                last.then_inc(yT_ps, 1)

            def post_logits(g):
                pe.wait_ge(yT_sb, g + 1)
                for i in range(IT):
                    last = nc.tensor.matmul(ps[:, Y_T, i * E:(i + 1) * E], yT[:, i * P:(i + 1) * P], wr_sb[:], start=True, stop=True)
                last.then_inc(lg_ps, 1)

            def post_ranks(g):
                pe.wait_ge(either_ok, g + 1)
                at = ps[:, Y_T, 64:64 + (IT + 1) * E]
                nc.tensor.matmul(at[:, 0:IT * E], before[:], either[:].rearrange("p i e -> p (i e)"), start=True, stop=False,
                                 skip_group_check=True)
                for k in range(1, IT + 1):
                    last = nc.tensor.matmul(at[:, k * E:(IT + 1) * E], onesb[:], either[:, 0:IT + 1 - k].rearrange("p i e -> p (i e)"),
                                            start=False, stop=(k == IT), skip_group_check=True)
                last.then_inc(rank_ps, 1)

            def group(g, first, last):
                for b in range(NB):
                    if b % 2 == 0 and not (last and b + AHEAD >= NB):
                        turn(g + (b + AHEAD) // NB, (b + AHEAD) % NB)
                        turn(g + (b + AHEAD) // NB, (b + AHEAD) % NB + 1)
                    add_up(g, b, first)
                    if not first:
                        if b == 17:
                            post_T(g - 1)
                        if b == 19:
                            post_logits(g - 1)
                        if b == 28:
                            post_ranks(g - 1)
                    if b == 20 and not last:
                        beta_rows(g + 1)
                    if last and 2 <= b < 2 + 2 * E and b % 2 == 0:
                        fold((b - 2) // 2)

            def fold(e):
                if e == 0:
                    pe.wait_ge(ld_w, 32)
                for j in range(HB):
                    last = nc.tensor.matmul(ps[:, BETA, e * HB + j:e * HB + j + 1],
                                            w1[:, e * H + j * P:e * H + (j + 1) * P], bcol[:, e:e + 1], start=True, stop=True)
                last.then_inc(lnb_ps, 1)

            beta_rows(0)
            for b in range(AHEAD):
                turn(0, b)
            group(0, True, False)
            with pe.Fori(1, G - 1) as g:
                group(g, False, False)
            group(G - 1, False, True)
            def rows_T(h, q):
                pe.wait_ge(xs_ld[q % XS], 16 * (UNROLL // XS) * h + 16 * (q // XS + 1))
                if not (isinstance(h, int) and UNROLL * h + q < 1):
                    pe.wait_ge(x_low, UNROLL * h + q)
                for a in range(2):
                    last = nc.tensor.transpose(ps[:, psX, a * P:(a + 1) * P], xs[:, q % XS, a, 0:D], ident[:])
                last.then_inc(x_turned, 1)

            def up(h, q):
                pe.wait_ge(w1_there, UNROLL * h + (q + 1))
                pe.wait_ge(x_low, UNROLL * h + (q + 1))
                if not (isinstance(h, int) and UNROLL * h + q < 2):
                    pe.wait_ge(h_gelu, UNROLL * h + (q - 1))
                for j in range(HB):
                    at = ps[:, psH + 2 * (q % 2) + j // 2, (j % 2) * TR:(j % 2 + 1) * TR]
                    for n, (part, rows) in enumerate(((0, xT_hi), (0, xT_lo), (1, xT_hi))):
                        last = nc.tensor.matmul(at, w1e[:, q % 2, part, j * P:(j + 1) * P], rows[:, q % 2],
                                                start=(n == 0), stop=(n == 2))
                last.then_inc(h_ps, 1)

            def down(h, q):
                e = pe.value_load(table[0:1, 0, bass.ds(UNROLL * h + q, 1)], min_val=0, max_val=E - 1)
                pe.wait_ge(h_gelu, UNROLL * h + (q + 1))
                if not (isinstance(h, int) and UNROLL * h + q < 2):
                    pe.wait_ge(y_added, UNROLL * h + (q - 1))
                for a in range(2):
                    for j in range(HB):
                        last = nc.tensor.matmul(ps[:, psY[q % 2], a * D:(a + 1) * D], hT[:, q % 2, j, a * P:(a + 1) * P],
                                                w2[:, bass.ds(e * H + j * D, D)], start=(j == 0), stop=(j == HB - 1))
                last.then_inc(y_ps, 1)

            pe.wait_ge(table_ok, 1)
            pe.wait_ge(sums_free, 2 * G + 2)
            rows_T(0, 0)
            rows_T(0, 1)
            up(0, 0)

            def step(h, q):
                if exists(h, q + 2):
                    rows_T(*shifted(h, q, 2))
                if exists(h, q + 1):
                    up(*shifted(h, q, 1))
                down(h, q)

            between = {3: (lambda: post_T(G - 1),), 4: (lambda: post_logits(G - 1),), 6: (lambda: post_ranks(G - 1),),
                      EARLY - 1: (lambda: pe.wait_ge(table_ok, 2),)}
            steps(pe, step, between)


_INS = ['x', 'adj', 'L0_gnn_context', 'L0_gnn_W_common', 'L0_gnn_w_left', 'L0_gnn_b_left', 'L0_gnn_w_right',
        'L0_gnn_b_right', 'L0_ffn_Wr', 'L0_ffn_br', 'L0_ffn_ln_g', 'L0_ffn_ln_b', 'L0_ffn_W1', 'L0_ffn_b1',
        'L0_ffn_W2', 'L0_ffn_b2']


def kernel(**inputs):
    import numpy as np
    import concourse.bacc as bacc
    from concourse.bass_utils import run_bass_kernel_spmd

    nc = bacc.Bacc("TRN2", target_bir_lowering=False, num_devices=1)
    arrays, args = {}, []
    for name in _INS:
        a = np.ascontiguousarray(inputs[name])
        if a.ndim == 0:
            a = a.reshape(1)
        arrays[f"in_{name}"] = a
        args.append(nc.dram_tensor(f"in_{name}", a.shape, mybir.dt.from_np(a.dtype), kind="ExternalInput").ap())
    args.append(nc.dram_tensor("out", (N, D), FP32, kind="ExternalOutput").ap())
    build(nc, *args)
    r = run_bass_kernel_spmd(nc, [arrays], core_ids=[0])
    return r.results[0]["out"]
```
